# Optimizing a Trainium2 kernel written in Bass

```python
import numpy as np
import jax
import jax.numpy as jnp

def _softmax(x, axis=-1):
    return jax.nn.softmax(x, axis=axis)

def _gelu(x):
    return jax.nn.gelu(x, approximate=True)

def _silu(x):
    return jax.nn.silu(x)

def _sigmoid(x):
    return jax.nn.sigmoid(x)

def _layernorm(x, axis=-1, eps=1e-05):
    m = jnp.mean(x, axis=axis, keepdims=True)
    v = jnp.var(x, axis=axis, keepdims=True)
    return (x - m) / jnp.sqrt(v + eps)

def _scatter_add(tgt, idx, src, axis=0):
    return tgt.at[idx].add(src)

def _segment_sum(src, seg, n):
    return jax.ops.segment_sum(src, seg, n)
kernel_name = 'mk_seq_postln_d1_jaxref_r8_af33ec'

def setup_inputs(seed: int=0):
    np.random.seed(seed)
    _w = jnp.asarray

    def _L0_attn_setup():
        import jax, jax.numpy as jnp
        import numpy as np
        B, S, D = (4, 512, 128)
        key = jax.random.key(seed)
        ks = jax.random.split(key, 7)
        scale = 1.0 / np.sqrt(D)
        return {'x': jax.random.normal(ks[0], (B, S, D), dtype=jnp.float32), 'W_in': jax.random.normal(ks[1], (D, D), dtype=jnp.float32) * scale, 'W_select': jax.random.normal(ks[2], (D, D), dtype=jnp.float32) * scale, 'W_gate': jax.random.normal(ks[3], (D, D), dtype=jnp.float32) * scale, 'W_out': jax.random.normal(ks[4], (D, D), dtype=jnp.float32) * scale, 'W_delta': jax.random.normal(ks[5], (D, D), dtype=jnp.float32) * scale, 'log_a': jax.random.normal(ks[6], (D,), dtype=jnp.float32) * 0.1}
    _L0_attn_in = _L0_attn_setup()

    def _L0_ffn_setup():
        import jax, jax.numpy as jnp
        import numpy as np
        TOPK = 8
        BN_EPS = 1e-05
        key = jax.random.key(seed)
        ks = jax.random.split(key, 5)
        b, n, d = (2, 128, 128)
        h, nk, kd = (8, 32, 128)
        ne = nk * nk
        scale = 0.02
        return {'inputs': jax.random.normal(ks[0], (b, n, d), jnp.float32), 'gamma': jnp.ones((d,), jnp.float32), 'beta': jnp.zeros((d,), jnp.float32), 'w_q': jax.random.normal(ks[1], (2 * h * kd, d), jnp.float32) * scale, 'keys': jax.random.normal(ks[2], (h, nk, 2, kd), jnp.float32) * scale, 'key_in': jax.random.normal(ks[3], (ne, d), jnp.float32) * scale, 'key_out': jax.random.normal(ks[4], (ne, d), jnp.float32) * scale}
    _L0_ffn_in = _L0_ffn_setup()
    _d = {'L0_attn_x': _L0_attn_in['x'], 'L0_attn_W_in': _L0_attn_in['W_in'], 'L0_attn_W_select': _L0_attn_in['W_select'], 'L0_attn_W_gate': _L0_attn_in['W_gate'], 'L0_attn_W_out': _L0_attn_in['W_out'], 'L0_attn_W_delta': _L0_attn_in['W_delta'], 'L0_attn_log_a': _L0_attn_in['log_a'], 'L0_ffn_gamma': _L0_ffn_in['gamma'], 'L0_ffn_beta': _L0_ffn_in['beta'], 'L0_ffn_w_q': _L0_ffn_in['w_q'], 'L0_ffn_keys': _L0_ffn_in['keys'], 'L0_ffn_key_in': _L0_ffn_in['key_in'], 'L0_ffn_key_out': _L0_ffn_in['key_out']}
    _x0 = _d['L0_attn_x']
    _d['L0_attn_x'] = jax.random.normal(jax.random.fold_in(jax.random.key(seed), 1), (4, 1024, 128), dtype=_x0.dtype)
    del _x0
    return _d

def reference(L0_attn_x, L0_attn_W_in, L0_attn_W_select, L0_attn_W_gate, L0_attn_W_out, L0_attn_W_delta, L0_attn_log_a, L0_ffn_gamma, L0_ffn_beta, L0_ffn_w_q, L0_ffn_keys, L0_ffn_key_in, L0_ffn_key_out):

    def _L0_attn_ref(x, W_in, W_select, W_gate, W_out, W_delta, log_a):
        import jax, jax.numpy as jnp
        import numpy as np
        B, S, D = (4, 512, 128)
        a_base = jax.nn.sigmoid(log_a).astype(x.dtype)
        delta = jnp.maximum(jax.nn.softplus(jnp.einsum('bsd,ed->bse', x, W_delta)), 0.0001)
        decay = jnp.exp(-delta * a_base)
        update = jax.nn.sigmoid(jnp.einsum('bsd,ed->bse', x, W_select)) * jnp.tanh(jnp.einsum('bsd,ed->bse', x, W_in))
        gate = jax.nn.sigmoid(jnp.einsum('bsd,ed->bse', x, W_gate))

        def step(state, inputs):
            dec_t, upd_t = inputs
            state = dec_t * state + upd_t
            return (state, state)
        init = jnp.zeros((x.shape[0], x.shape[2]), dtype=x.dtype)
        _, states = jax.lax.scan(step, init, (decay.transpose(1, 0, 2), update.transpose(1, 0, 2)))
        states = states.transpose(1, 0, 2)
        out = gate * states
        y = jnp.einsum('bsd,ed->bse', out, W_out)
        return y

    def _L0_ffn_ref(inputs, gamma, beta, w_q, keys, key_in, key_out):
        import jax, jax.numpy as jnp
        import numpy as np
        TOPK = 8
        BN_EPS = 1e-05
        b, n, d = inputs.shape
        h, nk, _, kd = keys.shape
        k = TOPK
        x = inputs.reshape(b * n, d)
        mu = jnp.mean(x, axis=0)
        var = jnp.mean(jnp.square(x - mu), axis=0)
        xn = (x - mu) * jax.lax.rsqrt(var + BN_EPS) * gamma + beta
        q = (xn @ w_q.T).reshape(b, n, 2, h, kd).transpose(2, 0, 1, 3, 4)
        sim = jnp.einsum('pbnhd,hkpd->pbnhk', q, keys)
        s, i = jax.lax.top_k(sim, k)
        sx, sy = (s[0], s[1])
        ix, iy = (i[0], i[1])
        all_scores = (sx[..., :, None] + sy[..., None, :]).reshape(b, n, h, k * k)
        all_idx = (ix[..., :, None] * nk + iy[..., None, :]).reshape(b, n, h, k * k)
        scores, pk = jax.lax.top_k(all_scores, k)
        idx = jnp.take_along_axis(all_idx, pk, axis=-1)
        w_down = key_in[idx]
        w_up = key_out[idx]
        o = jnp.einsum('bnd,bnhkd->bnhk', inputs, w_down)
        o = jax.nn.gelu(o, approximate=False) * jax.nn.softmax(scores, axis=-1)
        return jnp.einsum('bnhk,bnhkd->bnd', o, w_up)
    x = L0_attn_x
    x = _layernorm(x + _L0_attn_ref(x, L0_attn_W_in, L0_attn_W_select, L0_attn_W_gate, L0_attn_W_out, L0_attn_W_delta, L0_attn_log_a), axis=-1)
    x = _layernorm(x + _L0_ffn_ref(x, L0_ffn_gamma, L0_ffn_beta, L0_ffn_w_q, L0_ffn_keys, L0_ffn_key_in, L0_ffn_key_out), axis=-1)
    return x

_drawn_inputs = setup_inputs


def setup_inputs(seed=0):
    import zlib

    import numpy as np

    out = dict(_drawn_inputs(seed))
    spreads = {'L0_ffn_gamma': (1.0, 0.6), 'L0_ffn_beta': (0.0, 0.8)}
    factors = {'L0_attn_log_a': 7.388,
     'L0_ffn_w_q': 8.0,
     'L0_ffn_keys': 8.0,
     'L0_ffn_key_in': 8.0,
     'L0_ffn_key_out': 8.0}
    for name, (base, spread) in spreads.items():
        noise = np.random.default_rng([zlib.crc32(name.encode()), seed]).standard_normal(out[name].shape)
        drawn = base * np.exp(spread * noise) if base else spread * noise
        out[name] = jnp.asarray(drawn.astype(out[name].dtype))
    for name, factor in factors.items():
        out[name] = (out[name] * factor).astype(out[name].dtype)
    return out
```

```python
from contextlib import ExitStack

import concourse.bass as bass
from concourse import mybir

ALU = mybir.AluOpType
ACT = mybir.ActivationFunctionType
AX_X = mybir.AxisListType.X
F32 = mybir.dt.float32
F16 = mybir.dt.float16
U16 = mybir.dt.uint16
U32 = mybir.dt.uint32
I32 = mybir.dt.int32

P = 128
LN_EPS = 1e-5
BN_EPS = 1e-5
W_SCALE = 2.0 ** 14
REPLACED = -3.0e38
CODE_BASE = 128


def seqffn_kernel(nc, x, w_in, w_select, w_gate, w_out, w_delta, log_a, gamma, beta, w_q, keys,
                  key_in, key_out, out):
    B, S, D = x.shape
    H, NK, _, KD = keys.shape
    NE = NK * NK
    TOPK = 8
    T = B * S // P
    CH = 4
    CW = CH * P
    NCH = T // CH
    HALVES = S // CW
    ROWS = 2 * H
    NCAND = 20
    SL = H * TOPK
    JL, JH = 4, NK // 4
    assert D == P and KD == P and NK == 32 and H == 8 and NE == JH * P

    x_v = x.rearrange("b (n p) d -> p (b n) d", p=P)
    out_v = out.rearrange("b (n p) d -> p (b n) d", p=P)

    with ExitStack() as ctx:
        def sb(name, shape, dt=F32):
            return ctx.enter_context(nc.sbuf_tensor(name, shape, dt))

        def sem(name):
            return ctx.enter_context(nc.semaphore(name))

        psum = ctx.enter_context(nc.psum_tensor("psum", [P, 8 * 512], F32))

        def bank(i):
            return psum[:, i * 512:(i + 1) * 512]

        ident = sb("ident", [P, P])
        ident16 = sb("ident16", [P, P], F16)
        iota_i = sb("iota_i", [P, 2, NK, 2], I32)
        iota = sb("iota", [P, 2, NK, 2], F16)
        eps = sb("eps", [P, 1])
        cols = sb("cols", [P, 3])
        a_base = sb("a_base", [P, 1])
        neg_a = sb("neg_a", [P, 1])
        nat = sb("nat", [P, 17, P])
        trn = sb("trn", [P, 17, P])
        wq = sb("wq", [P, ROWS, P])
        ko = sb("ko", [P, JH, P])
        msim = sb("msim", [P, ROWS * NK])
        xs = sb("xs", [P, 2, CH, P])
        shared = sb("shared", [P, 9, 2, CW])
        xT, absd, lnd, sp, decay, tin, sel, gate, states = (shared[:, i] for i in range(9))
        st1 = sb("st1", [P, T, 6])
        mv1 = sb("mv1", [P, T, 2])
        rstd1 = sb("rstd1", [P, T])
        x1 = sb("x1", [P, T, P])
        x1T = sb("x1T", [P, (T + 2) * P])
        bst = sb("bst", [P, NCH, 6])
        bmv = sb("bmv", [P, 2])
        bsd = sb("bsd", [P, 1])
        bsc = sb("bsc", [P, 2])
        xn = sb("xn", [P, 2, P])
        sims = sb("sims", [P, 2, ROWS, NK])
        vals = sb("vals", [P, ROWS, TOPK])
        idx = sb("idx", [P, ROWS, TOPK], U32)
        ixf = sb("ixf", [P, H, TOPK])
        cand = sb("cand", [P, H, NCAND])
        code = sb("code", [P, H, NCAND])
        top = sb("top", [P, H, TOPK])
        dif = sb("dif", [P, H, NCAND])
        ex = sb("ex", [P, H * NCAND])
        marked = sb("marked", [P, H, NCAND])
        words = sb("words", [P, 2, H, NCAND])
        picked = sb("picked", [P, 2, H, TOPK])
        exk = sb("exk", [P, H, TOPK])
        zsum = sb("zsum", [P, H])
        zinv = sb("zinv", [P, H])
        wk = sb("wk", [P, H, TOPK])
        codes = sb("codes", [P, 2, SL], U16)
        lists = sb("lists", [P, 4, 2, SL], F16)
        listsT = sb("listsT", [P, 4, P], F16)
        hotx = sb("hotx", [P, 2, P // 2, NK, 2], F16)
        hoty = sb("hoty", [P, P // 2, NK, 2], F16)
        hotw = sb("hotw", [P, 2, 2, P // 2, NK, 2], F16)
        pev = shared[:, 0:4].rearrange("p a b w -> p (a b w)").rearrange("p (j t) -> p j t", j=NK)
        pt = sb("pt", [P, JH, CW])
        gl = shared[:, 4:8].rearrange("p a b w -> p (a b) w")
        zf = sb("zf", [P, CH, P])
        st2 = sb("st2", [P, CH, 6])
        mv2 = sb("mv2", [P, CH, 2])
        rstd2 = sb("rstd2", [P, CH])
        outb = sb("outb", [P, CH, P])

        words16 = words[:, :, :, :].rearrange("p w h c -> p w (h c)").bitcast(U16).rearrange(
            "p w (c s) -> p w c s", s=2)
        picked16 = picked[:, :, :, :].rearrange("p w h k -> p w (h k)").bitcast(U16).rearrange(
            "p w (k s) -> p w k s", s=2)
        ex16 = ex[:, :].bitcast(U16).rearrange("p (c s) -> p s c", s=2)
        exk16 = exk[:, :, :].rearrange("p h k -> p (h k)").bitcast(U16).rearrange(
            "p (k s) -> p s k", s=2)
        b_xT, b_delta, b_in, b_sel, b_gate, b_y1 = (bank(i) for i in range(6))
        b_w = (bank(6), bank(7))
        b_sim, b_g, b_y2 = bank(4), bank(5), bank(6)
        b_lists = bank(7)[:, 0:256].bitcast(F16)

        names = """passed iota_done ld_w ld_keys ld_rest ld_x0 ld_x1 c_ident c_iota c_misc
            w_trn w_evac m_mm m_evac c_cols c_nega
            xT_mm xT_evac z_delta z_in z_sel z_gate ln_done sp_raw sp_done decay_done tin_done
            sel_done gate_done upd_done scan_done gated y1_mm x1_sum st1_done mv1_done sd1 rstd1_done
            nrm x1T_mm x1T_evac bst_done x1_copy bmv_done bsd_done bsd_inv bsc_half bsc_mu bsc_done
            xn_done sim_mm sims_ready vals_done idx_done ixf_done cand_done top_done dif_done ex_done
            lo_done code_done marked_done hi_done picked_done exk_done codes_done z_done zinv_done
            wk_done whi_done wlo_done conv_done lists_mm lists_evac hoty_done hot_done hotlo_done
            p_mm p_evac relaid g_mm gelu_done a_done y2_mm zf_done st2_done mv2_done sd2 rstd2_done
            out_done stored""".split()
        s = {n: sem(n) for n in names}

        block = ctx.enter_context(nc.Block())

        def wait(eng, name, value):
            if isinstance(value, int) and value <= 0:
                return
            eng.wait_ge(s[name], value)

        def hold(eng, name, value):
            wait(eng, name, value)
            if not isinstance(value, int):
                eng.sem_inc(s["passed"], 1)

        @block.sync
        def _(sp_eng):
            for n, w in enumerate((w_delta, w_in, w_select, w_gate, w_out)):
                sp_eng.dma_start(nat[:, n, :], w).then_inc(s["ld_w"], 16)
            def batch_row(b):
                for k in range(HALVES):
                    wait(sp_eng, "x1_sum", b * 2)
                    wait(sp_eng, "xT_mm", b * 2)
                    sp_eng.dma_start(xs[:, k, :, :], x_v[:, bass.ds(b * (2 * CH) + k * CH, CH), :]).then_inc(
                        s[f"ld_x{k}"], 16)

            batch_row(0)
            with sp_eng.Fori(1, B) as b:
                batch_row(b)
            def relayout(q):
                hold(sp_eng, "p_evac", q * 4 + 4)
                wait(sp_eng, "a_done", q * JH)
                for c in range(4):
                    for jl in range(JL):
                        sp_eng.dma_start(pt[32 * jl:32 * jl + 32, :, c * P:(c + 1) * P],
                                         pev[32 * c:32 * c + 32, jl * JH:(jl + 1) * JH, :]).then_inc(s["relaid"], 16)

            def store(q):
                wait(sp_eng, "out_done", q + 1)
                sp_eng.dma_start(out_v[:, bass.ds(q * CH, CH), :], outb[:, :, :]).then_inc(s["stored"], 16)

            relayout(0)
            with sp_eng.Fori(2, NCH) as q:
                store(q - 2)
                relayout(q - 1)
            store(NCH - 2)
            relayout(NCH - 1)
            store(NCH - 1)
            sp_eng.wait_ge(s["stored"], 16 * NCH)

        @block.gpsimd
        def _(pool):
            pool.memset(ident[:, :], 0.0)
            pool.memset(ident16[:, :], 0.0)
            pool.memset(eps[:, :], LN_EPS)
            pool.memset(x1T[:, T * P:(T + 2) * P], 0.0).then_inc(s["c_misc"], 1)
            pool.wait_ge(s["c_misc"], 1)
            for m in (ident, ident16):
                pool.affine_select(out=m[:, :], in_=m[:, :], compare_op=ALU.not_equal, fill=1.0, base=0,
                                   pattern=[[-1, P]], channel_multiplier=1).then_inc(s["c_ident"], 1)
            pool.iota(iota_i[:, 0], pattern=[[NK, NK], [0, 2]], base=0, channel_multiplier=0)
            pool.iota(iota_i[:, 1], pattern=[[1, NK], [0, 2]], base=0, channel_multiplier=0).then_inc(s["c_iota"], 1)
            def chunk_pair(b):
                for k in range(2):
                    wait(pool, "nrm", b * 2 + (k + 1))
                    pool.tensor_copy(x1[:, bass.ds(b * (2 * CH) + k * CH, CH), :], xs[:, k, :, :]).then_inc(s["x1_copy"], 1)

            chunk_pair(0)
            with pool.Fori(1, NCH // 2) as b:
                chunk_pair(b)
            def low_parts(q):
                for par in range(2):
                    for hf in range(2):
                        g = slice(32 * hf, 32 * hf + 32)
                        wait(pool, "hoty_done", q * 4 + (par * 2 + hf + 1))
                        if hf == 0:
                            wait(pool, "p_mm", q * 2 + (par - 1))
                        w_lo = listsT[:, 3, 64 * hf:64 * hf + 64].rearrange("p (g s) -> p g s", s=2)
                        pool.tensor_tensor(
                            hotw[:, par, 1, g, :, :], hoty[:, g, :, :],
                            w_lo.unsqueeze(2).to_broadcast([P, 32, NK, 2]), ALU.mult).then_inc(s["hotlo_done"], 1)

            low_parts(0)
            with pool.Fori(1, T // 4) as q:
                low_parts(q)
        @block.scalar
        def _(act):
            act.dma_start(cols[:, 0:1], log_a.rearrange("(d o) -> d o", o=1)).then_inc(s["ld_rest"], 16)
            act.dma_start(cols[:, 1:2], gamma.rearrange("(d o) -> d o", o=1)).then_inc(s["ld_rest"], 16)
            act.dma_start(cols[:, 2:3], beta.rearrange("(d o) -> d o", o=1)).then_inc(s["ld_rest"], 16)
            for g in range(2):
                act.dma_start(nat[:, 5 + 2 * g:7 + 2 * g, :],
                              keys[4 * g:4 * g + 4].rearrange("h k p d -> (h k) p d")).then_inc(s["ld_keys"], 16)
            for jl in range(JL):
                for dst, src in ((nat[32 * jl:32 * jl + 32, 9:17, :], key_in), (ko[32 * jl:32 * jl + 32, :, :], key_out)):
                    act.dma_start(dst, src.rearrange("(i l h) d -> l i h d", l=JL, h=JH)[jl]).then_inc(s["ld_keys"], 16)
            act.dma_start(wq[:, :, :], w_q.rearrange("(r k) d -> k r d", k=P)).then_inc(s["ld_keys"], 16)

            def weights_out(g):
                n = min(4, 17 - 4 * g)
                act.wait_ge(s["w_trn"], g + 1)
                act.activation(trn[:, 4 * g:4 * g + n, :], b_w[g % 2][:, 0:n * P], ACT.Copy).then_inc(s["w_evac"], 1)

            act.wait_ge(s["ld_rest"], 48)
            act.activation(a_base[:, :], cols[:, 0:1], ACT.Sigmoid).then_inc(s["c_cols"], 1)
            act.wait_ge(s["c_cols"], 1)
            act.mul(neg_a[:, :], a_base[:, :], -1.0).then_inc(s["c_nega"], 1)
            weights_out(0)
            weights_out(1)
            act.wait_ge(s["c_nega"], 1)
            def batch_row(b):
                for k in range(2):
                    wait(act, "z_delta", b * 2 + (k + 1))
                    wait(act, "sp_raw", b * 2)
                    act.activation(absd[:, k], b_delta, ACT.Abs).then_inc(s["decay_done"], 1)
                    wait(act, "decay_done", b * 8 + (3 * k + 1))
                    act.activation(sp[:, k], absd[:, k], ACT.Exp, scale=-1.0).then_inc(s["decay_done"], 1)
                    wait(act, "decay_done", b * 8 + (3 * k + 2))
                    act.activation(lnd[:, k], sp[:, k], ACT.Ln, bias=1.0).then_inc(s["decay_done"], 1)
                    wait(act, "decay_done", b * 8 + (3 * k + 3))
                    act.nop().then_inc(s["ln_done"], 1)
                for k in range(2):
                    wait(act, "sp_done", b * 2 + (k + 1))
                    wait(act, "scan_done", b * 2)
                    act.activation(decay[:, k], sp[:, k], ACT.Exp, scale=neg_a[:, 0:1]).then_inc(s["decay_done"], 1)
                for k in range(2):
                    wait(act, "gated", b * 2)
                    wait(act, "z_in", b * 2 + (k + 1))
                    act.activation(tin[:, k], b_in, ACT.Tanh).then_inc(s["tin_done"], 1)
                    wait(act, "z_sel", b * 2 + (k + 1))
                    act.activation(sel[:, k], b_sel, ACT.Sigmoid).then_inc(s["sel_done"], 1)
                    wait(act, "z_gate", b * 2 + (k + 1))
                    act.activation(gate[:, k], b_gate, ACT.Sigmoid).then_inc(s["gate_done"], 1)

            batch_row(0)
            with act.Fori(1, B) as b:
                batch_row(b)
            for g in range(2, 5):
                weights_out(g)
            act.wait_ge(s["m_mm"], 1)
            act.activation(msim[:, :], b_w[1], ACT.Copy).then_inc(s["m_evac"], 1)
            act.wait_ge(s["mv1_done"], 6)
            act.wait_ge(s["c_misc"], 1)
            act.activation(rstd1[:, :], mv1[:, :, 1], ACT.Sqrt, bias=eps[:, 0:1]).then_inc(s["sd1"], 1)
            def chunk_pair(b):
                for k in range(2):
                    wait(act, "x1T_mm", b * 2 + (k + 1))
                    act.activation(x1T[:, bass.ds(b * (2 * CW) + k * CW, CW)], b_in if k else b_delta,
                                   ACT.Copy).then_inc(s["x1T_evac"], 1)

            chunk_pair(0)
            with act.Fori(1, NCH // 2) as b:
                chunk_pair(b)
            act.wait_ge(s["bmv_done"], 1)
            act.activation(bsd[:, :], bmv[:, 1:2], ACT.Sqrt, bias=eps[:, 0:1]).then_inc(s["bsd_done"], 1)
            act.wait_ge(s["bsc_done"], 1)
            act.wait_ge(s["x1T_evac"], NCH)

            def normed(n, par):
                wait(act, "sim_mm", n - 1)
                act.activation(xn[:, par], x1T[:, bass.ds(n * P, P)], ACT.Identity,
                               bias=bsc[:, 1:2], scale=bsc[:, 0:1]).then_inc(s["xn_done"], 1)

            def sims_out(n, par):
                wait(act, "sim_mm", n + 1)
                wait(act, "idx_done", n - 1)
                act.activation(sims[:, par].rearrange("p r k -> p (r k)"), b_sim, ACT.Copy).then_inc(s["sims_ready"], 1)

            def exps(n, par):
                wait(act, "dif_done", n + 1)
                wait(act, "lo_done", n)
                act.activation(ex[:, :], dif[:, :, :].rearrange("p h c -> p (h c)"), ACT.Exp).then_inc(s["ex_done"], 1)
                wait(act, "ex_done", n + 1)
                wait(act, "picked_done", n)
                act.activation(words16[:, :, :, 0], ex16, ACT.Copy).then_inc(s["lo_done"], 1)

            def convert(n, par, m):
                wait(act, "codes_done", n + 1)
                wait(act, "lists_mm", m)
                act.activation(lists[:, 0:2, par, :], codes[:, :, :], ACT.Copy).then_inc(s["conv_done"], 1)

            def lists_out(m):
                wait(act, "lists_mm", m + 1)
                wait(act, "hot_done", m * 2)
                wait(act, "hotlo_done", m * 2)
                act.activation(listsT[:, :, :].rearrange("p f t -> p (f t)"), b_lists, ACT.Copy).then_inc(s["lists_evac"], 1)

            def p_out(q, t):
                wait(act, "p_mm", q * 2 + (t // 2 + 1))
                wait(act, "relaid", q * 256)
                src = psum[:, 1024 * (t % 2):1024 * (t % 2) + 1024].rearrange("p (g j) -> p j g", g=32)
                act.activation(pev[:, :, 32 * t:32 * t + 32], src, ACT.Copy, scale=1.0 / W_SCALE).then_inc(s["p_evac"], 1)

            def gelus(q):
                for jh in range(JH):
                    wait(act, "g_mm", q * JH + (jh + 1))
                    wait(act, "y2_mm", q)
                    act.activation(gl[:, jh], b_g, ACT.Gelu).then_inc(s["gelu_done"], 1)

            def spread2(q):
                wait(act, "mv2_done", q + 1)
                wait(act, "out_done", q)
                act.activation(rstd2[:, :], mv2[:, :, 1], ACT.Sqrt, bias=eps[:, 0:1]).then_inc(s["sd2"], 1)

            def quad(q, pair_before, quad_before):
                for t in range(4):
                    n, par = q * 4 + t, t % 2
                    exps(n, par)
                    sims_out(n + 1, 1 - par)
                    normed(n + 2, par)
                    convert(n, par, q * 2 + t // 2)
                    if t == 0 and quad_before:
                        spread2(q - 2)
                    if t == 2:
                        lists_out(q * 2)
                        if pair_before:
                            p_out(q - 1, 2)
                            p_out(q - 1, 3)
                            gelus(q - 1)
                p_out(q, 0)
                p_out(q, 1)
                lists_out(q * 2 + 1)

            normed(0, 0)
            normed(1, 1)
            sims_out(0, 0)
            quad(0, False, False)
            quad(1, True, False)
            quad(2, True, True)
            with act.Fori(3, NCH) as q:
                quad(q, True, True)
            spread2(NCH - 2)
            p_out(NCH - 1, 2)
            p_out(NCH - 1, 3)
            gelus(NCH - 1)
            spread2(NCH - 1)

        @block.vector
        def _(dve):
            dve.wait_ge(s["c_iota"], 1)
            dve.tensor_copy(iota[:, :, :, :], iota_i[:, :, :, :]).then_inc(s["iota_done"], 1)
            def batch_row(b):
                for k in range(2):
                    wait(dve, "xT_mm", b * 2 + (k + 1))
                    wait(dve, "z_gate", b * 2)
                    dve.tensor_copy(xT[:, k], b_xT).then_inc(s["xT_evac"], 1)
                for k in range(2):
                    wait(dve, "ln_done", b * 2 + (k + 1))
                    dve.scalar_tensor_tensor(out=absd[:, k], in0=b_delta, scalar=0.0, in1=lnd[:, k],
                                             op0=ALU.max, op1=ALU.add).then_inc(s["sp_raw"], 1)
                    wait(dve, "sp_raw", b * 2 + (k + 1))
                    dve.tensor_scalar(sp[:, k], absd[:, k], 1e-4, None, ALU.max).then_inc(s["sp_done"], 1)
                for k in range(2):
                    wait(dve, "tin_done", b * 2 + (k + 1))
                    wait(dve, "sel_done", b * 2 + (k + 1))
                    dve.tensor_tensor(tin[:, k], tin[:, k], sel[:, k], ALU.mult).then_inc(s["upd_done"], 1)
                    wait(dve, "upd_done", b * 2 + (k + 1))
                    wait(dve, "decay_done", b * 8 + (7 + k))
                    dve.tensor_tensor_scan(states[:, k], decay[:, k], tin[:, k],
                                           0.0 if k == 0 else states[:, 0, CW - 1:CW],
                                           ALU.mult, ALU.add).then_inc(s["scan_done"], 1)
                    wait(dve, "scan_done", b * 2 + (k + 1))
                    wait(dve, "gate_done", b * 2 + (k + 1))
                    wait(dve, "y1_mm", b * 2)
                    dve.tensor_tensor(sel[:, k], states[:, k], gate[:, k], ALU.mult).then_inc(s["gated"], 1)
                for k in range(2):
                    wait(dve, "y1_mm", b * 2 + (k + 1))
                    at = b * (2 * CH) + k * CH
                    dve.tensor_tensor(x1[:, bass.ds(at, CH), :], b_y1.rearrange("p (t d) -> p t d", t=CH), xs[:, k],
                                      ALU.add).then_inc(s["x1_sum"], 1)
                    wait(dve, "x1_sum", b * 2 + (k + 1))
                    for t in range(CH):
                        dve.bn_stats(st1[:, bass.ds(at + t, 1), :], x1[:, bass.ds(at + t, 1), :]).then_inc(s["st1_done"], 1)

            batch_row(0)
            with dve.Fori(1, B) as b:
                batch_row(b)
            dve.wait_ge(s["st1_done"], T)
            dve.tensor_tensor(mv1[:, :, 0], st1[:, :, 1], st1[:, :, 4], ALU.add).then_inc(s["mv1_done"], 1)
            dve.tensor_tensor(mv1[:, :, 1], st1[:, :, 1], st1[:, :, 4], ALU.subtract).then_inc(s["mv1_done"], 1)
            dve.tensor_tensor(rstd1[:, :], st1[:, :, 2], st1[:, :, 5], ALU.add).then_inc(s["mv1_done"], 1)
            dve.wait_ge(s["mv1_done"], 3)
            dve.tensor_scalar(mv1[:, :, 0], mv1[:, :, 0], 0.5, None, ALU.mult).then_inc(s["mv1_done"], 1)
            dve.scalar_tensor_tensor(out=mv1[:, :, 1], in0=mv1[:, :, 1], scalar=0.25, in1=mv1[:, :, 1],
                                     op0=ALU.mult, op1=ALU.mult).then_inc(s["mv1_done"], 1)
            dve.wait_ge(s["mv1_done"], 5)
            dve.scalar_tensor_tensor(out=mv1[:, :, 1], in0=rstd1[:, :], scalar=1.0 / D, in1=mv1[:, :, 1],
                                     op0=ALU.mult, op1=ALU.add).then_inc(s["mv1_done"], 1)
            dve.wait_ge(s["sd1"], 1)
            dve.reciprocal(rstd1[:, :], rstd1[:, :]).then_inc(s["rstd1_done"], 1)
            dve.wait_ge(s["rstd1_done"], 1)
            def chunk_pair(b):
                for k in range(2):
                    wait(dve, "x1T_mm", b * 2)
                    wait(dve, "x1_copy", b * 2)
                    for t in range(CH):
                        n = b * (2 * CH) + (k * CH + t)
                        last = dve.tensor_scalar(xs[:, k, t:t + 1, :], x1[:, bass.ds(n, 1), :], mv1[:, bass.ds(n, 1), 0],
                                                 rstd1[:, bass.ds(n, 1)], ALU.subtract, ALU.mult)
                    last.then_inc(s["nrm"], 1)
                for k in range(2):
                    wait(dve, "x1T_evac", b * 2 + (k + 1))
                    dve.bn_stats(bst[:, bass.ds(b * 2 + k, 1), :], b_in if k else b_delta).then_inc(s["bst_done"], 1)

            chunk_pair(0)
            with dve.Fori(1, NCH // 2) as b:
                chunk_pair(b)
            dve.wait_ge(s["bst_done"], NCH)
            dve.bn_aggr(bmv[:, :], bst[:, :, :]).then_inc(s["bmv_done"], 1)
            dve.wait_ge(s["bsd_done"], 1)
            dve.reciprocal(bsd[:, :], bsd[:, :]).then_inc(s["bsd_inv"], 1)
            dve.wait_ge(s["bsd_inv"], 1)
            dve.tensor_tensor(bsc[:, 0:1], bsd[:, :], cols[:, 1:2], ALU.mult).then_inc(s["bsc_half"], 1)
            dve.wait_ge(s["bsc_half"], 1)
            dve.tensor_tensor(bsd[:, :], bsc[:, 0:1], bmv[:, 0:1], ALU.mult).then_inc(s["bsc_mu"], 1)
            dve.wait_ge(s["bsc_mu"], 1)
            dve.tensor_tensor(bsc[:, 1:2], cols[:, 2:3], bsd[:, :], ALU.subtract).then_inc(s["bsc_done"], 1)

            def select(n, par, m):
                sim = sims[:, par]
                hold(dve, "sims_ready", n + 1)
                for r in range(ROWS):
                    last = dve.max(vals[:, r, :], sim[:, r, :])
                last.then_inc(s["vals_done"], 1)
                hold(dve, "vals_done", n + 1)
                for r in range(ROWS):
                    last = dve.max_index(idx[:, r, :], vals[:, r, :], sim[:, r, :])
                last.then_inc(s["idx_done"], 1)
                vx, vy = vals[:, 0:H, :], vals[:, H:ROWS, :]
                dve.tensor_tensor(cand[:, :, 0:8], vx[:, :, 0:1].to_broadcast([P, H, 8]), vy[:, :, :], ALU.add)
                dve.tensor_tensor(cand[:, :, 8:12], vx[:, :, 1:2].to_broadcast([P, H, 4]), vy[:, :, 0:4], ALU.add)
                dve.tensor_tensor(cand[:, :, 12:16].rearrange("p h (a b) -> p h a b", a=2),
                                  vx[:, :, 2:4].unsqueeze(3).to_broadcast([P, H, 2, 2]),
                                  vy[:, :, 0:2].unsqueeze(2).to_broadcast([P, H, 2, 2]), ALU.add)
                dve.tensor_tensor(cand[:, :, 16:20], vx[:, :, 4:8], vy[:, :, 0:1].to_broadcast([P, H, 4]),
                                  ALU.add).then_inc(s["cand_done"], 1)
                wait(dve, "idx_done", n + 1)
                iy = idx[:, H:ROWS, :]
                dve.tensor_scalar(ixf[:, :, :], idx[:, 0:H, :], float(CODE_BASE), None, ALU.add).then_inc(s["ixf_done"], 1)
                hold(dve, "cand_done", n + 1)
                for h in range(H):
                    last = dve.max(top[:, h, :], cand[:, h, :])
                last.then_inc(s["top_done"], 1)
                wait(dve, "ixf_done", n + 1)
                for lo, hi, a, yb in ((0, 8, 0, iy), (8, 12, 1, iy[:, :, 0:4]), (12, 14, 2, iy[:, :, 0:2]),
                                      (14, 16, 3, iy[:, :, 0:2])):
                    dve.scalar_tensor_tensor(out=code[:, :, lo:hi], in0=ixf[:, :, a:a + 1].to_broadcast([P, H, hi - lo]),
                                             scalar=float(NK), in1=yb, op0=ALU.mult, op1=ALU.add)
                dve.scalar_tensor_tensor(out=code[:, :, 16:20], in0=ixf[:, :, 4:8], scalar=float(NK),
                                         in1=iy[:, :, 0:1].to_broadcast([P, H, 4]), op0=ALU.mult,
                                         op1=ALU.add).then_inc(s["code_done"], 1)
                wait(dve, "ex_done", n)
                wait(dve, "top_done", n + 1)
                dve.tensor_tensor(dif[:, :, :], cand[:, :, :], top[:, :, 0:1].to_broadcast([P, H, NCAND]),
                                  ALU.subtract).then_inc(s["dif_done"], 1)
                for h in range(H):
                    last = dve.match_replace(marked[:, h, :], top[:, h, :], cand[:, h, :], REPLACED)
                last.then_inc(s["marked_done"], 1)
                wait(dve, "code_done", n + 1)
                wait(dve, "marked_done", n + 1)
                for w in range(2):
                    last = dve.scalar_tensor_tensor(
                        out=words16[:, w, :, 1],
                        in0=marked[:, :, :].rearrange("p h c -> p (h c)"), scalar=REPLACED / 2,
                        in1=code[:, :, :].rearrange("p h c -> p (h c)"),
                        op0=ALU.is_lt, op1=ALU.mult)
                last.then_inc(s["hi_done"], 1)
                wait(dve, "lo_done", n + 1)
                hold(dve, "hi_done", n + 1)
                for w in range(2):
                    for h in range(H):
                        last = dve.max(picked[:, w, h, :], words[:, w, h, :])
                last.then_inc(s["picked_done"], 1)
                wait(dve, "conv_done", n)
                wait(dve, "picked_done", n + 1)
                dve.tensor_copy(exk16, picked16[:, :, :, 0]).then_inc(s["exk_done"], 1)
                dve.tensor_scalar(codes[:, 0, :], picked16[:, 0, :, 1], NK * (NK - 1), None, ALU.bitwise_and)
                dve.tensor_scalar(codes[:, 1, :], picked16[:, 0, :, 1], NK - 1, None,
                                  ALU.bitwise_and).then_inc(s["codes_done"], 1)
                wait(dve, "exk_done", n + 1)
                dve.reduce_sum(zsum[:, :], exk[:, :, :], AX_X).then_inc(s["z_done"], 1)
                wait(dve, "z_done", n + 1)
                dve.reciprocal(zinv[:, :], zsum[:, :]).then_inc(s["zinv_done"], 1)
                wait(dve, "zinv_done", n + 1)
                dve.scalar_tensor_tensor(out=wk[:, :, :], in0=exk[:, :, :], scalar=W_SCALE,
                                         in1=zinv[:, :].unsqueeze(2).to_broadcast([P, H, TOPK]), op0=ALU.mult,
                                         op1=ALU.mult).then_inc(s["wk_done"], 1)
                wait(dve, "lists_mm", m)
                wait(dve, "wk_done", n + 1)
                flat = wk[:, :, :].rearrange("p h k -> p (h k)")
                dve.tensor_copy(lists[:, 2, par, :], flat).then_inc(s["whi_done"], 1)
                wait(dve, "whi_done", n + 1)
                dve.tensor_tensor(lists[:, 3, par, :], flat, lists[:, 2, par, :], ALU.subtract).then_inc(s["wlo_done"], 1)

            def one_hots(m, par):
                if isinstance(m, int):
                    wait(dve, "iota_done", 1)
                wait(dve, "lists_evac", m + 1)
                wait(dve, "p_mm", m - 1)
                for hf in range(2):
                    g = slice(32 * hf, 32 * hf + 32)

                    def spread(f):
                        v = listsT[:, f, 64 * hf:64 * hf + 64].rearrange("p (g s) -> p g s", s=2)
                        return v.unsqueeze(2).to_broadcast([P, 32, NK, 2])

                    wait(dve, "hotlo_done", m * 2 - 1 + hf)
                    dve.tensor_tensor(hoty[:, g], iota[:, 1].unsqueeze(1).to_broadcast([P, 32, NK, 2]), spread(1),
                                      ALU.is_equal).then_inc(s["hoty_done"], 1)
                    dve.tensor_tensor(hotx[:, par, g], iota[:, 0].unsqueeze(1).to_broadcast([P, 32, NK, 2]), spread(0),
                                      ALU.is_equal)
                    wait(dve, "hoty_done", m * 2 + (hf + 1))
                    dve.tensor_tensor(hotw[:, par, 0, g], hoty[:, g], spread(2), ALU.mult).then_inc(s["hot_done"], 1)

            def weigh(q):
                wait(dve, "relaid", q * 256 + 256)
                for jh in range(JH):
                    wait(dve, "gelu_done", q * JH + (jh + 1))
                    by_token = gl[:, jh].rearrange("p (t c g) -> p t c g", t=CH, c=4)
                    dve.tensor_tensor(by_token, pt[:, jh].rearrange("p (c t g) -> p t c g", c=4, t=CH), by_token,
                                      ALU.mult).then_inc(s["a_done"], 1)

            def residual(q):
                wait(dve, "y2_mm", q + 1)
                dve.tensor_tensor(zf[:, :, :], b_y2.rearrange("p (t d) -> p t d", t=CH), x1[:, bass.ds(q * CH, CH), :],
                                  ALU.add).then_inc(s["zf_done"], 1)
                wait(dve, "zf_done", q + 1)
                for t in range(CH):
                    last = dve.bn_stats(st2[:, t, :], zf[:, t, :])
                last.then_inc(s["st2_done"], 1)
                hold(dve, "st2_done", q + 1)
                for t in range(CH):
                    last = dve.bn_aggr(mv2[:, t, :], st2[:, t, :])
                last.then_inc(s["mv2_done"], 1)

            def norm_out(q):
                wait(dve, "sd2", q + 1)
                dve.reciprocal(rstd2[:, :], rstd2[:, :]).then_inc(s["rstd2_done"], 1)
                wait(dve, "rstd2_done", q + 1)
                wait(dve, "stored", q * 16)
                for t in range(CH):
                    last = dve.tensor_scalar(outb[:, t, :], zf[:, t, :], mv2[:, t, 0:1], rstd2[:, t:t + 1],
                                             ALU.subtract, ALU.mult)
                last.then_inc(s["out_done"], 1)

            def quad(q, pair_before, quad_before):
                select(q * 4, 0, q * 2)
                if quad_before:
                    residual(q - 2)
                if pair_before:
                    one_hots(q * 2 - 1, 1)
                select(q * 4 + 1, 1, q * 2)
                if quad_before:
                    norm_out(q - 2)
                select(q * 4 + 2, 0, q * 2 + 1)
                one_hots(q * 2, 0)
                select(q * 4 + 3, 1, q * 2 + 1)
                if pair_before:
                    weigh(q - 1)

            quad(0, False, False)
            quad(1, True, False)
            quad(2, True, True)
            with dve.Fori(3, NCH) as q:
                quad(q, True, True)
            residual(NCH - 2)
            one_hots(T // 2 - 1, 1)
            norm_out(NCH - 2)
            weigh(NCH - 1)
            residual(NCH - 1)
            norm_out(NCH - 1)

        @block.tensor
        def _(pe):
            def weights(g):
                if g >= 2:
                    pe.wait_ge(s["w_evac"], g - 1)
                for n in range(4 * g, min(4 * g + 4, 17)):
                    last = pe.transpose(b_w[g % 2][:, (n % 4) * P:(n % 4 + 1) * P], nat[:, n, :], ident[:, :])
                last.then_inc(s["w_trn"], 1)

            pe.wait_ge(s["c_ident"], 2)
            pe.wait_ge(s["ld_w"], 80)
            weights(0)
            pe.wait_ge(s["ld_keys"], 16 * 11)
            weights(1)
            pe.wait_ge(s["w_evac"], 2)
            def batch_row(b):
                for k in range(2):
                    wait(pe, f"ld_x{k}", b * 16 + 16)
                    wait(pe, "xT_evac", b * 2 + k)
                    for t in range(CH):
                        last = pe.transpose(b_xT[:, t * P:(t + 1) * P], xs[:, k, t, :], ident[:, :])
                    last.then_inc(s["xT_mm"], 1)
                    wait(pe, "xT_evac", b * 2 + (k + 1))
                    for n, (to, done, used) in enumerate(((b_delta, "z_delta", "sp_raw"), (b_in, "z_in", "tin_done"),
                                                          (b_sel, "z_sel", "sel_done"), (b_gate, "z_gate", "gate_done"))):
                        wait(pe, used, b * 2 + k)
                        pe.matmul(to, trn[:, n, :], xT[:, k], start=True, stop=True).then_inc(s[done], 1)
                for k in range(2):
                    wait(pe, "gated", b * 2 + (k + 1))
                    wait(pe, "x1_sum", b * 2 + k)
                    for t in range(CH):
                        last = pe.matmul(b_y1[:, t * P:(t + 1) * P], sel[:, k, t * P:(t + 1) * P], trn[:, 4, :],
                                         start=True, stop=True)
                    last.then_inc(s["y1_mm"], 1)

            batch_row(0)
            with pe.Fori(1, B) as b:
                batch_row(b)
            for g in range(2, 5):
                weights(g)
            pe.wait_ge(s["w_evac"], 5)
            for r in range(ROWS):
                p, h = r // H, r % H
                last = pe.matmul(b_w[1][:, r * NK:(r + 1) * NK], wq[:, r, :],
                                 trn[:, 5 + 2 * (h // 4) + p, (h % 4) * NK:(h % 4 + 1) * NK], start=True, stop=True)
            last.then_inc(s["m_mm"], 1)
            def chunk_pair(b):
                for k in range(2):
                    wait(pe, "nrm", b * 2 + (k + 1))
                    wait(pe, "x1T_evac", b * 2)
                    wait(pe, "bst_done", b * 2)
                    to = b_in if k else b_delta
                    for t in range(CH):
                        last = pe.transpose(to[:, t * P:(t + 1) * P], xs[:, k, t, :], ident[:, :])
                    last.then_inc(s["x1T_mm"], 1)

            chunk_pair(0)
            with pe.Fori(1, NCH // 2) as b:
                chunk_pair(b)
            pe.wait_ge(s["m_evac"], 1)
            pe.wait_ge(s["x1T_evac"], NCH)

            def scores(n, par):
                wait(pe, "xn_done", n + 1)
                wait(pe, "sims_ready", n)
                pe.matmul(b_sim, xn[:, par], msim[:, :], start=True, stop=True).then_inc(s["sim_mm"], 1)

            def lists_turned(m):
                wait(pe, "conv_done", m * 2 + 2)
                wait(pe, "wlo_done", m * 2 + 2)
                wait(pe, "lists_evac", m)
                for f in range(4):
                    last = pe.transpose(b_lists[:, f * P:(f + 1) * P],
                                        lists[:, f, :, :].rearrange("p t s -> p (t s)"), ident16[:, :])
                last.then_inc(s["lists_mm"], 1)

            def scatter(m, par):
                hold(pe, "p_evac", m * 2)
                for hf in range(2):
                    wait(pe, "hot_done", m * 2 + (hf + 1))
                    hold(pe, "hotlo_done", m * 2 + (hf + 1))
                    for g in range(32):
                        for c in (2 * hf, 2 * hf + 1):
                            tok = 32 * c + g
                            for tile in range(2):
                                rows = slice(64 * tile, 64 * tile + 64)
                                at = 1024 * tile + NK * g
                                for part in range(2):
                                    last = pe.matmul(psum[32 * c:32 * c + 32, at:at + NK],
                                                     hotx[rows, par, tok // 2, :, tok % 2],
                                                     hotw[rows, par, part, tok // 2, :, tok % 2],
                                                     start=(part == 0), stop=(part == 1))
                last.then_inc(s["p_mm"], 1)

            def experts_in(q):
                for jh in range(JH):
                    wait(pe, "gelu_done", q * JH + jh)
                    pe.matmul(b_g, trn[:, 9 + jh, :],
                              x1T[:, bass.ds(q * CW, CW)], start=True, stop=True).then_inc(s["g_mm"], 1)

            def experts_out(q):
                wait(pe, "a_done", q * JH + JH)
                wait(pe, "zf_done", q)
                for t in range(CH):
                    for jh in range(JH):
                        last = pe.matmul(b_y2[:, t * P:(t + 1) * P],
                                         gl[:, jh, t * P:(t + 1) * P], ko[:, jh, :], start=(jh == 0), stop=(jh == JH - 1))
                last.then_inc(s["y2_mm"], 1)

            def quad(q, pair_before):
                scores(q * 4 + 1, 1)
                scores(q * 4 + 2, 0)
                if pair_before:
                    scatter(q * 2 - 1, 1)
                lists_turned(q * 2)
                scores(q * 4 + 3, 1)
                scores(q * 4 + 4, 0)
                if pair_before:
                    experts_in(q - 1)
                scatter(q * 2, 0)
                lists_turned(q * 2 + 1)
                if pair_before:
                    experts_out(q - 1)

            scores(0, 0)
            quad(0, False)
            quad(1, True)
            with pe.Fori(2, NCH) as q:
                quad(q, True)
            scatter(T // 2 - 1, 1)
            experts_in(NCH - 1)
            experts_out(NCH - 1)


_INS = ['L0_attn_x', 'L0_attn_W_in', 'L0_attn_W_select', 'L0_attn_W_gate', 'L0_attn_W_out', 'L0_attn_W_delta',
        'L0_attn_log_a', 'L0_ffn_gamma', 'L0_ffn_beta', 'L0_ffn_w_q', 'L0_ffn_keys', 'L0_ffn_key_in',
        'L0_ffn_key_out']


def kernel(**inputs):
    import numpy as _np
    import concourse.bacc as _bacc
    from concourse import mybir as _mybir
    from concourse.bass_utils import run_bass_kernel_spmd as _run

    nc = _bacc.Bacc("TRN2", target_bir_lowering=False, num_devices=1)
    arrays, args = {}, []
    for name in _INS:
        a = _np.ascontiguousarray(inputs[name])
        arrays[f"in_{name}_dram"] = a
        args.append(nc.dram_tensor(f"in_{name}_dram", a.shape, _mybir.dt.from_np(a.dtype), kind="ExternalInput").ap())
    shape = inputs['L0_attn_x'].shape
    args.append(nc.dram_tensor("out_0_dram", shape, _mybir.dt.float32, kind="ExternalOutput").ap())
    seqffn_kernel(nc, *args)
    r = _run(nc, [arrays], core_ids=[0])
    return r.results[0]["out_0_dram"]
```

```python
from contextlib import ExitStack

import concourse.bass as bass
from concourse import mybir

ALU = mybir.AluOpType
ACT = mybir.ActivationFunctionType
AX_X = mybir.AxisListType.X
F32 = mybir.dt.float32
F16 = mybir.dt.float16
U16 = mybir.dt.uint16
U32 = mybir.dt.uint32
I32 = mybir.dt.int32

P = 128
LN_EPS = 1e-5
BN_EPS = 1e-5
W_SCALE = 2.0 ** 14
REPLACED = -3.0e38
CODE_BASE = 128


def seqffn_kernel(nc, x, w_in, w_select, w_gate, w_out, w_delta, log_a, gamma, beta, w_q, keys,
                  key_in, key_out, out):
    B, S, D = x.shape
    H, NK, _, KD = keys.shape
    NE = NK * NK
    TOPK = 8
    T = B * S // P
    CH = 4
    CW = CH * P
    NCH = T // CH
    GR = 4
    NG = NCH // GR
    ROW_CH = S // CW
    ROWS = 2 * H
    NCAND = 20
    SL = H * TOPK
    JL, JH = 4, NK // 4
    assert D == P and KD == P and NK == 32 and H == 8 and NE == JH * P and GR % ROW_CH == 0

    x_v = x.rearrange("b (n p) d -> p (b n) d", p=P)
    out_v = out.rearrange("b (n p) d -> p (b n) d", p=P)

    with ExitStack() as ctx:
        def sb(name, shape, dt=F32):
            return ctx.enter_context(nc.sbuf_tensor(name, shape, dt))

        def sem(name):
            return ctx.enter_context(nc.semaphore(name))

        psum = ctx.enter_context(nc.psum_tensor("psum", [P, 8 * 512], F32))

        def bank(i):
            return psum[:, i * 512:(i + 1) * 512]

        ident = sb("ident", [P, P])
        ident16 = sb("ident16", [P, P], F16)
        iota_i = sb("iota_i", [P, 2, NK, 2], I32)
        iota = sb("iota", [P, 2, NK, 2], F16)
        eps = sb("eps", [P, 1])
        cols = sb("cols", [P, 3])
        a_base = sb("a_base", [P, 1])
        neg_a = sb("neg_a", [P, 1])
        nat = sb("nat", [P, 17, P])
        trn = sb("trn", [P, 17, P])
        wq = sb("wq", [P, ROWS, P])
        ko = sb("ko", [P, JH, P])
        msim = sb("msim", [P, ROWS * NK])
        xs = sb("xs", [P, GR, CH, P])
        arena = sb("arena", [P, 27648])
        xT, absd, ex1, lnd, relu, sp, decay, tin, sel, gate, states, outg = (
            arena[:, i * GR * CW:(i + 1) * GR * CW].rearrange("p (k w) -> p k w", k=GR) for i in range(12))
        st1 = sb("st1", [P, T, 6])
        mv1 = sb("mv1", [P, T, 2])
        rstd1 = sb("rstd1", [P, T])
        x1 = sb("x1", [P, T, P])
        x1T = sb("x1T", [P, (T + 4) * P])
        bst = sb("bst", [P, NCH, 6])
        bmv = sb("bmv", [P, 2])
        bsd = sb("bsd", [P, 1])
        bsc = sb("bsc", [P, 2])
        RH = 2 * H
        xn = sb("xn", [P, 2, P])
        sims = sb("sims", [P, 2, ROWS, NK])
        vals = sb("vals", [P, 2, RH, TOPK])
        idx = sb("idx", [P, 2, RH, TOPK], U32)
        ixf = sb("ixf", [P, RH, TOPK])
        iyf = sb("iyf", [P, RH, TOPK])
        cand = sb("cand", [P, RH, NCAND])
        code = sb("code", [P, RH, NCAND])
        top = sb("top", [P, RH, TOPK])
        dif = sb("dif", [P, RH, NCAND])
        ex = sb("ex", [P, RH * NCAND])
        marked = sb("marked", [P, RH, NCAND])
        words = sb("words", [P, 2, RH, NCAND])
        picked = sb("picked", [P, 2, RH, TOPK])
        exk = sb("exk", [P, RH, TOPK])
        zsum = sb("zsum", [P, RH])
        zinv = sb("zinv", [P, RH])
        wk = sb("wk", [P, RH, TOPK])
        codes = sb("codes", [P, 2, 2 * SL], U16)
        lists = sb("lists", [P, 4, 2 * SL], F16)
        listsT = sb("listsT", [P, 4, P], F16)
        HW = P // 2 * NK
        pev = arena[:, 0:NK * P].rearrange("p (j t) -> p j t", j=NK)
        gl = arena[:, 4096:8192].rearrange("p (j w) -> p j w", j=JH)
        pt = arena[:, 8192:12288].rearrange("p (j w) -> p j w", j=JH)
        hots = arena[:, 12288:12288 + 7 * HW].bitcast(F16)
        hoty = hots[:, 0:2 * HW].rearrange("p (t k s) -> p t k s", k=NK, s=2)
        hotx = hots[:, 2 * HW:6 * HW].rearrange("p (b t k s) -> p b t k s", b=2, k=NK, s=2)
        hotw = hots[:, 6 * HW:14 * HW].rearrange("p (b w t k s) -> p b w t k s", b=2, w=2, k=NK, s=2)
        zf = nat[:, 0:CH, :]
        st2 = sb("st2", [P, CH, 6])
        mv2 = sb("mv2", [P, CH, 2])
        rstd2 = sb("rstd2", [P, CH])
        outb = nat[:, CH:2 * CH, :]

        words16 = words[:, :, :, :].rearrange("p w h c -> p w (h c)").bitcast(U16).rearrange(
            "p w (c s) -> p w c s", s=2)
        picked16 = picked[:, :, :, :].rearrange("p w h k -> p w (h k)").bitcast(U16).rearrange(
            "p w (k s) -> p w k s", s=2)
        ex16 = ex[:, :].bitcast(U16).rearrange("p (c s) -> p s c", s=2)
        exk16 = exk[:, :, :].rearrange("p h k -> p (h k)").bitcast(U16).rearrange(
            "p (k s) -> p s k", s=2)
        b_xT, b_delta, b_in, b_sel, b_gate, b_y1 = bank(0), (bank(1), bank(2)), bank(3), bank(4), bank(5), bank(6)
        b_w, b_m = (bank(7), bank(6), bank(7), bank(0), bank(7)), bank(0)
        b_x1T = tuple(bank(1 + i) for i in range(GR))
        b_sim, b_y2 = (bank(4), bank(5)), bank(6)
        b_g = tuple(bank(i) for i in range(4))
        b_lists = bank(7)[:, 0:256].bitcast(F16)

        names = """passed iota_done ld_w ld_wout ld_keys ld_rest ld_x ld_x0 ld_x1 ld_x2 ld_x3 c_ident c_iota c_misc
            w_trn w_evac m_mm m_evac c_cols c_nega
            xT_mm xT_evac z_delta z_in z_sel z_gate abs_done relu_done e_done ln_done sp_raw sp_done decay_done
            tin_done sel_done gate_done upd_done scan_done gated y1_mm x1_sum st1_done mv1_done sd1 rstd1_done
            nrm x1T_mm x1T_evac bst_done x1_copy bmv_done bsd_done bsd_inv bsc_half bsc_mu bsc_done
            xn_done sim_mm sims_ready vals_done idx_done ixf_done cand_done top_done dif_done ex_done
            lo_done code_done marked_done hi_done picked_done exk_done codes_done z_done zinv_done
            wk_done whi_done wlo_done conv_done lists_mm lists_evac hoty_done hot_done hotlo_done
            p_mm p_evac relaid g_mm gelu_done a_done y2_mm zf_done st2_done mv2_done sd2 rstd2_done
            out_done stored""".split()
        s = {n: sem(n) for n in names}

        W_GROUPS = ((0, 4), (4, 5), (5, 9), (9, 13), (13, 17))

        block = ctx.enter_context(nc.Block())

        def wait(eng, name, value):
            if isinstance(value, int) and value <= 0:
                return
            eng.wait_ge(s[name], value)

        def hold(eng, name, value):
            wait(eng, name, value)
            if not isinstance(value, int):
                eng.sem_inc(s["passed"], 1)

        @block.sync
        def _(sp_eng):
            def group(g):
                for k in range(GR):
                    wait(sp_eng, "xT_mm", g * GR + (k + 1 - GR))
                    sp_eng.dma_start(xs[:, k, :, :], x_v[:, bass.ds(g * (GR * CH) + k * CH, CH), :]).then_inc(
                        s[f"ld_x{k}"], 16)
                    if k == 0 and isinstance(g, int):
                        for n, w in enumerate((w_delta, w_in, w_select, w_gate)):
                            sp_eng.dma_start(nat[:, n, :], w).then_inc(s["ld_w"], 16)

            group(0)
            for k in range(B):
                n = T // B
                sp_eng.dma_start(x1[:, k * n:(k + 1) * n, :], x_v[:, k * n:(k + 1) * n, :]).then_inc(s["ld_x"], 16)
            with sp_eng.Fori(1, NG) as g:
                group(g)
            for g in range(2):
                sp_eng.dma_start(nat[:, 5 + 2 * g:7 + 2 * g, :],
                                 keys[4 * g:4 * g + 4].rearrange("h k p d -> (h k) p d")).then_inc(s["ld_keys"], 16)
            for jl in range(JL):
                for dst, src in ((nat[32 * jl:32 * jl + 32, 9:17, :], key_in), (ko[32 * jl:32 * jl + 32, :, :], key_out)):
                    sp_eng.dma_start(dst, src.rearrange("(i l h) d -> l i h d", l=JL, h=JH)[jl]).then_inc(s["ld_keys"], 16)
            sp_eng.dma_start(wq[:, :, :], w_q.rearrange("(r k) d -> k r d", k=P)).then_inc(s["ld_keys"], 16)

            def relayout(q):
                hold(sp_eng, "p_evac", q * 4 + 4)
                wait(sp_eng, "a_done", q * JH)
                for c in range(4):
                    for jl in range(JL):
                        sp_eng.dma_start(pt[32 * jl:32 * jl + 32, :, c * P:(c + 1) * P],
                                         pev[32 * c:32 * c + 32, jl * JH:(jl + 1) * JH, :]).then_inc(s["relaid"], 16)

            def store(q):
                wait(sp_eng, "out_done", q + 1)
                sp_eng.dma_start(out_v[:, bass.ds(q * CH, CH), :], outb[:, :, :]).then_inc(s["stored"], 16)

            relayout(0)
            with sp_eng.Fori(1, NCH) as q:
                relayout(q)
                store(q - 1)
            store(NCH - 1)
            sp_eng.wait_ge(s["stored"], 16 * NCH)

        @block.gpsimd
        def _(pool):
            pool.memset(ident[:, :], 0.0)
            pool.memset(ident16[:, :], 0.0)
            pool.memset(eps[:, :], LN_EPS)
            pool.memset(x1T[:, T * P:(T + 4) * P], 0.0).then_inc(s["c_misc"], 1)
            pool.wait_ge(s["c_misc"], 1)
            for m in (ident, ident16):
                pool.affine_select(out=m[:, :], in_=m[:, :], compare_op=ALU.not_equal, fill=1.0, base=0,
                                   pattern=[[-1, P]], channel_multiplier=1).then_inc(s["c_ident"], 1)
            pool.iota(iota_i[:, 0], pattern=[[NK, NK], [0, 2]], base=0, channel_multiplier=0)
            pool.iota(iota_i[:, 1], pattern=[[1, NK], [0, 2]], base=0, channel_multiplier=0).then_inc(s["c_iota"], 1)
            def update(g, k):
                c = g * GR + k
                wait(pool, "tin_done", c + 1)
                wait(pool, "sel_done", c + 1)
                pool.tensor_tensor(tin[:, k], tin[:, k], sel[:, k], ALU.mult).then_inc(s["upd_done"], 1)

            def gate_out(g, k):
                c = g * GR + k
                wait(pool, "scan_done", c + 1)
                wait(pool, "gate_done", c + 1)
                wait(pool, "y1_mm", c + 1 - GR)
                pool.tensor_tensor(outg[:, k], states[:, k], gate[:, k], ALU.mult).then_inc(s["gated"], 1)

            for k in range(GR):
                update(0, k)
            with pool.Fori(1, NG) as g:
                for k in range(GR):
                    gate_out(g - 1, k)
                    update(g, k)
            for k in range(GR):
                gate_out(NG - 1, k)

            def x1_back(g):
                for k in range(GR):
                    wait(pool, "nrm", g * GR + (k + 1))
                    pool.tensor_copy(x1[:, bass.ds(g * (GR * CH) + k * CH, CH), :], xs[:, k, :, :]).then_inc(s["x1_copy"], 1)

            x1_back(0)
            with pool.Fori(1, NG) as g:
                x1_back(g)
            def low_part(m, par, hf):
                g = slice(32 * hf, 32 * hf + 32)
                wait(pool, "hoty_done", m * 2 + (hf + 1))
                if hf == 0:
                    wait(pool, "p_mm", m - 1)
                w_lo = listsT[:, 3, 64 * hf:64 * hf + 64].rearrange("p (g s) -> p g s", s=2)
                pool.tensor_tensor(
                    hotw[:, par, 1, g, :, :], hoty[:, g, :, :],
                    w_lo.unsqueeze(2).to_broadcast([P, 32, NK, 2]), ALU.mult).then_inc(s["hotlo_done"], 1)

            def candidate_codes(m):
                hold(pool, "idx_done", m * 2 + 2)
                pool.tensor_copy(iyf[:, :, :], idx[:, 1])
                pool.tensor_scalar(ixf[:, :, :], idx[:, 0], float(CODE_BASE), float(NK), ALU.add, ALU.mult).then_inc(
                    s["ixf_done"], 1)
                wait(pool, "ixf_done", m + 1)
                wait(pool, "hi_done", m)
                iy = iyf[:, :, :]
                pool.tensor_tensor(code[:, :, 0:8], ixf[:, :, 0:1].to_broadcast([P, RH, 8]), iy, ALU.add)
                pool.tensor_tensor(code[:, :, 8:12], ixf[:, :, 1:2].to_broadcast([P, RH, 4]), iy[:, :, 0:4], ALU.add)
                pool.tensor_tensor(code[:, :, 12:16].rearrange("p h (a b) -> p h a b", a=2),
                                   ixf[:, :, 2:4].unsqueeze(3).to_broadcast([P, RH, 2, 2]),
                                   iy[:, :, 0:2].unsqueeze(2).to_broadcast([P, RH, 2, 2]), ALU.add)
                pool.tensor_tensor(code[:, :, 16:20], ixf[:, :, 4:8], iy[:, :, 0:1].to_broadcast([P, RH, 4]),
                                   ALU.add).then_inc(s["code_done"], 1)

            def weigh(q):
                wait(pool, "relaid", q * 256 + 256)
                for jh in range(JH):
                    wait(pool, "gelu_done", q * JH + (jh + 1))
                    by_token = gl[:, jh].rearrange("p (t c g) -> p t c g", t=CH, c=4)
                    pool.tensor_tensor(by_token, pt[:, jh].rearrange("p (c t g) -> p t c g", c=4, t=CH), by_token,
                                       ALU.mult).then_inc(s["a_done"], 1)

            def quad(q, before):
                candidate_codes(q * 2)
                if before:
                    low_part(q * 2 - 1, 1, 0)
                    low_part(q * 2 - 1, 1, 1)
                candidate_codes(q * 2 + 1)
                low_part(q * 2, 0, 0)
                low_part(q * 2, 0, 1)
                if before:
                    weigh(q - 1)

            quad(0, False)
            with pool.Fori(1, NCH) as q:
                quad(q, True)
            low_part(T // 2 - 1, 1, 0)
            low_part(T // 2 - 1, 1, 1)
            weigh(NCH - 1)

        @block.scalar
        def _(act):
            act.dma_start(cols[:, 0:1], log_a.rearrange("(d o) -> d o", o=1)).then_inc(s["ld_rest"], 16)
            act.dma_start(cols[:, 1:2], gamma.rearrange("(d o) -> d o", o=1)).then_inc(s["ld_rest"], 16)
            act.dma_start(cols[:, 2:3], beta.rearrange("(d o) -> d o", o=1)).then_inc(s["ld_rest"], 16)
            act.dma_start(nat[:, 4, :], w_out).then_inc(s["ld_wout"], 16)

            def weights_out(g):
                lo, hi = W_GROUPS[g]
                act.wait_ge(s["w_trn"], g + 1)
                act.activation(trn[:, lo:hi, :], b_w[g][:, 0:(hi - lo) * P], ACT.Copy).then_inc(s["w_evac"], 1)

            weights_out(0)
            act.wait_ge(s["ld_rest"], 48)
            act.activation(a_base[:, :], cols[:, 0:1], ACT.Sigmoid).then_inc(s["c_cols"], 1)
            weights_out(1)
            act.wait_ge(s["c_cols"], 1)
            act.mul(neg_a[:, :], a_base[:, :], -1.0).then_inc(s["c_nega"], 1)

            def gates(g):
                for k in range(GR):
                    c = g * GR + k
                    wait(act, "z_delta", c + 1)
                    wait(act, "e_done", g)
                    act.activation(absd[:, k], b_delta[k % 2], ACT.Abs).then_inc(s["abs_done"], 1)
                    wait(act, "z_in", c + 1)
                    wait(act, "scan_done", c + 1 - GR)
                    act.activation(tin[:, k], b_in, ACT.Tanh).then_inc(s["tin_done"], 1)
                    wait(act, "z_sel", c + 1)
                    wait(act, "upd_done", c + 1 - GR)
                    act.activation(sel[:, k], b_sel, ACT.Sigmoid).then_inc(s["sel_done"], 1)
                    wait(act, "z_gate", c + 1)
                    wait(act, "gated", c + 1 - GR)
                    act.activation(gate[:, k], b_gate, ACT.Sigmoid).then_inc(s["gate_done"], 1)

            def decays(g):
                wait(act, "abs_done", g * GR + GR)
                wait(act, "ln_done", g * GR)
                act.activation(ex1, absd, ACT.Exp, scale=-1.0).then_inc(s["e_done"], 1)
                wait(act, "e_done", g + 1)
                for k in range(GR):
                    wait(act, "sp_raw", g * GR + (k + 1 - GR))
                    act.activation(lnd[:, k], ex1[:, k], ACT.Ln, bias=1.0).then_inc(s["ln_done"], 1)
                for k in range(GR):
                    c = g * GR + k
                    wait(act, "sp_done", c + 1)
                    wait(act, "scan_done", c + 1 - GR)
                    act.activation(decay[:, k], sp[:, k], ACT.Exp, scale=neg_a[:, 0:1]).then_inc(s["decay_done"], 1)

            act.wait_ge(s["c_nega"], 1)
            gates(0)
            decays(0)
            with act.Fori(1, NG) as g:
                gates(g)
                decays(g)
            for g in range(2, 5):
                weights_out(g)
            act.wait_ge(s["m_mm"], 1)
            act.activation(msim[:, :], b_m, ACT.Copy).then_inc(s["m_evac"], 1)
            act.wait_ge(s["mv1_done"], 6)
            act.wait_ge(s["c_misc"], 1)
            act.activation(rstd1[:, :], mv1[:, :, 1], ACT.Sqrt, bias=eps[:, 0:1]).then_inc(s["sd1"], 1)

            def x1T_out(g):
                for k in range(GR):
                    wait(act, "x1T_mm", g * GR + (k + 1))
                    act.activation(x1T[:, bass.ds(g * (GR * CW) + k * CW, CW)], b_x1T[k], ACT.Copy).then_inc(
                        s["x1T_evac"], 1)

            x1T_out(0)
            with act.Fori(1, NG) as g:
                x1T_out(g)
            act.wait_ge(s["bmv_done"], 1)
            act.activation(bsd[:, :], bmv[:, 1:2], ACT.Sqrt, bias=eps[:, 0:1]).then_inc(s["bsd_done"], 1)
            act.wait_ge(s["bsc_done"], 1)
            act.wait_ge(s["x1T_evac"], NCH)

            def normed(m):
                wait(act, "sim_mm", m * 2)
                for t in range(2):
                    last = act.activation(xn[:, t], x1T[:, bass.ds(m * (2 * P) + t * P, P)], ACT.Identity,
                                          bias=bsc[:, 1:2], scale=bsc[:, 0:1])
                    last.then_inc(s["xn_done"], 1)

            def sims_out(m):
                for t in range(2):
                    wait(act, "sim_mm", m * 2 + (t + 1))
                    wait(act, "idx_done", m * 2 - 1 + t)
                    act.activation(sims[:, t].rearrange("p r k -> p (r k)"), b_sim[t], ACT.Copy).then_inc(
                        s["sims_ready"], 1)

            def exps(m):
                wait(act, "dif_done", m + 1)
                wait(act, "lo_done", m)
                act.activation(ex[:, :], dif[:, :, :].rearrange("p h c -> p (h c)"), ACT.Exp).then_inc(s["ex_done"], 1)
                wait(act, "ex_done", m + 1)
                wait(act, "picked_done", m)
                act.activation(words16[:, :, :, 0], ex16, ACT.Copy).then_inc(s["lo_done"], 1)

            def convert(m):
                wait(act, "codes_done", m + 1)
                wait(act, "lists_mm", m)
                act.activation(lists[:, 0:2, :], codes[:, :, :], ACT.Copy).then_inc(s["conv_done"], 1)

            def lists_out(m):
                wait(act, "lists_mm", m + 1)
                wait(act, "hot_done", m * 2)
                wait(act, "hotlo_done", m * 2)
                act.activation(listsT[:, :, :].rearrange("p f t -> p (f t)"), b_lists, ACT.Copy).then_inc(s["lists_evac"], 1)

            def p_out(q, pair):
                wait(act, "p_mm", q * 2 + (pair + 1))
                if pair == 0:
                    wait(act, "relaid", q * 256)
                for t in range(2):
                    src = psum[:, 1024 * t:1024 * t + 1024].rearrange("p (g j) -> p j g", g=32)
                    at = 64 * pair + 32 * t
                    act.activation(pev[:, :, at:at + 32], src, ACT.Copy, scale=1.0 / W_SCALE).then_inc(s["p_evac"], 1)

            def gelus(q):
                wait(act, "y2_mm", q)
                for jh in range(JH):
                    wait(act, "g_mm", q * JH + (jh + 1))
                    act.activation(gl[:, jh], b_g[jh % 4], ACT.Gelu).then_inc(s["gelu_done"], 1)

            def spread2(q):
                wait(act, "mv2_done", q + 1)
                wait(act, "out_done", q)
                act.activation(rstd2[:, :], mv2[:, :, 1], ACT.Sqrt, bias=eps[:, 0:1]).then_inc(s["sd2"], 1)

            def quad(q, before, before2):
                if before:
                    lists_out(q * 2 - 1)
                    p_out(q - 1, 0)
                exps(q * 2)
                sims_out(q * 2 + 1)
                normed(q * 2 + 2)
                convert(q * 2)
                lists_out(q * 2)
                if before2:
                    spread2(q - 2)
                if before:
                    p_out(q - 1, 1)
                    gelus(q - 1)
                exps(q * 2 + 1)
                sims_out(q * 2 + 2)
                normed(q * 2 + 3)
                convert(q * 2 + 1)

            normed(0)
            sims_out(0)
            normed(1)
            quad(0, False, False)
            quad(1, True, False)
            quad(2, True, True)
            with act.Fori(3, NCH) as q:
                quad(q, True, True)
            lists_out(T // 2 - 1)
            p_out(NCH - 1, 0)
            spread2(NCH - 2)
            p_out(NCH - 1, 1)
            gelus(NCH - 1)
            spread2(NCH - 1)

        @block.vector
        def _(dve):
            dve.wait_ge(s["c_iota"], 1)
            dve.tensor_copy(iota[:, :, :, :], iota_i[:, :, :, :]).then_inc(s["iota_done"], 1)

            def evac_x(g, k):
                c = g * GR + k
                wait(dve, "xT_mm", c + 1)
                wait(dve, "z_gate", c + 1 - GR)
                dve.tensor_copy(xT[:, k], b_xT).then_inc(s["xT_evac"], 1)

            def positive_part(g, k):
                c = g * GR + k
                wait(dve, "abs_done", c + 1)
                wait(dve, "sp_raw", c + 1 - GR)
                dve.tensor_scalar(relu[:, k], b_delta[k % 2], 0.0, None, ALU.max).then_inc(s["relu_done"], 1)

            def softplus(g, k):
                c = g * GR + k
                wait(dve, "ln_done", c + 1)
                wait(dve, "relu_done", c + 1)
                wait(dve, "decay_done", c + 1 - GR)
                dve.tensor_tensor(sp[:, k], relu[:, k], lnd[:, k], ALU.add).then_inc(s["sp_raw"], 1)
                wait(dve, "sp_raw", c + 1)
                dve.tensor_scalar(sp[:, k], sp[:, k], 1e-4, None, ALU.max).then_inc(s["sp_done"], 1)

            def scan(g, k):
                c = g * GR + k
                wait(dve, "upd_done", c + 1)
                wait(dve, "decay_done", c + 1)
                wait(dve, "gated", c + 1 - GR)
                wait(dve, "scan_done", c)
                dve.tensor_tensor_scan(states[:, k], decay[:, k], tin[:, k],
                                       0.0 if k % ROW_CH == 0 else states[:, k - 1, CW - 1:CW],
                                       ALU.mult, ALU.add).then_inc(s["scan_done"], 1)

            def add_y(g, k):
                c = g * GR + k
                wait(dve, "y1_mm", c + 1)
                mine = x1[:, bass.ds(g * (GR * CH) + k * CH, CH), :]
                dve.tensor_tensor(mine, b_y1.rearrange("p (t d) -> p t d", t=CH), mine, ALU.add).then_inc(s["x1_sum"], 1)
                wait(dve, "x1_sum", c + 1)
                for t in range(CH):
                    tile = bass.ds(g * (GR * CH) + (k * CH + t), 1)
                    dve.bn_stats(st1[:, tile, :], x1[:, tile, :]).then_inc(s["st1_done"], 1)

            evac_x(0, 0)
            for k in range(GR):
                if k + 1 < GR:
                    evac_x(0, k + 1)
                positive_part(0, k)
            for k in range(GR):
                softplus(0, k)
            dve.wait_ge(s["ld_x"], 16 * B)
            with dve.Fori(1, NG) as g:
                evac_x(g, 0)
                for k in range(GR):
                    if k + 1 < GR:
                        evac_x(g, k + 1)
                    scan(g - 1, k)
                    positive_part(g, k)
                for k in range(GR):
                    add_y(g - 1, k)
                    softplus(g, k)
            for k in range(GR):
                scan(NG - 1, k)
            for k in range(GR):
                add_y(NG - 1, k)
            dve.wait_ge(s["st1_done"], T)
            dve.tensor_tensor(mv1[:, :, 0], st1[:, :, 1], st1[:, :, 4], ALU.add).then_inc(s["mv1_done"], 1)
            dve.tensor_tensor(mv1[:, :, 1], st1[:, :, 1], st1[:, :, 4], ALU.subtract).then_inc(s["mv1_done"], 1)
            dve.tensor_tensor(rstd1[:, :], st1[:, :, 2], st1[:, :, 5], ALU.add).then_inc(s["mv1_done"], 1)
            dve.wait_ge(s["mv1_done"], 3)
            dve.tensor_scalar(mv1[:, :, 0], mv1[:, :, 0], 0.5, None, ALU.mult).then_inc(s["mv1_done"], 1)
            dve.scalar_tensor_tensor(out=mv1[:, :, 1], in0=mv1[:, :, 1], scalar=0.25, in1=mv1[:, :, 1],
                                     op0=ALU.mult, op1=ALU.mult).then_inc(s["mv1_done"], 1)
            dve.wait_ge(s["mv1_done"], 5)
            dve.scalar_tensor_tensor(out=mv1[:, :, 1], in0=rstd1[:, :], scalar=1.0 / D, in1=mv1[:, :, 1],
                                     op0=ALU.mult, op1=ALU.add).then_inc(s["mv1_done"], 1)
            dve.wait_ge(s["sd1"], 1)
            dve.reciprocal(rstd1[:, :], rstd1[:, :]).then_inc(s["rstd1_done"], 1)
            dve.wait_ge(s["rstd1_done"], 1)

            def norm_x1(g, k):
                wait(dve, "x1T_mm", g * GR + (k + 1 - GR))
                wait(dve, "x1_copy", g * GR + (k + 1 - GR))
                for t in range(CH):
                    n = g * (GR * CH) + (k * CH + t)
                    last = dve.tensor_scalar(xs[:, k, t:t + 1, :], x1[:, bass.ds(n, 1), :], mv1[:, bass.ds(n, 1), 0],
                                             rstd1[:, bass.ds(n, 1)], ALU.subtract, ALU.mult)
                last.then_inc(s["nrm"], 1)

            def batch_stats(g, k):
                wait(dve, "x1T_evac", g * GR + (k + 1))
                dve.bn_stats(bst[:, bass.ds(g * GR + k, 1), :], b_x1T[k]).then_inc(s["bst_done"], 1)

            def norm_group(g):
                for k in range(GR):
                    norm_x1(g, k)
                    if k >= 2:
                        batch_stats(g, k - 2)
                batch_stats(g, GR - 2)
                batch_stats(g, GR - 1)

            norm_group(0)
            with dve.Fori(1, NG) as g:
                norm_group(g)
            dve.wait_ge(s["bst_done"], NCH)
            dve.bn_aggr(bmv[:, :], bst[:, :, :]).then_inc(s["bmv_done"], 1)
            dve.wait_ge(s["bsd_done"], 1)
            dve.reciprocal(bsd[:, :], bsd[:, :]).then_inc(s["bsd_inv"], 1)
            dve.wait_ge(s["bsd_inv"], 1)
            dve.tensor_tensor(bsc[:, 0:1], bsd[:, :], cols[:, 1:2], ALU.mult).then_inc(s["bsc_half"], 1)
            dve.wait_ge(s["bsc_half"], 1)
            dve.tensor_tensor(bsd[:, :], bsc[:, 0:1], bmv[:, 0:1], ALU.mult).then_inc(s["bsc_mu"], 1)
            dve.wait_ge(s["bsc_mu"], 1)
            dve.tensor_tensor(bsc[:, 1:2], cols[:, 2:3], bsd[:, :], ALU.subtract).then_inc(s["bsc_done"], 1)

            def hot_slice(hf):
                return slice(32 * hf, 32 * hf + 32)

            def spread(f, hf):
                v = listsT[:, f, 64 * hf:64 * hf + 64].rearrange("p (g s) -> p g s", s=2)
                return v.unsqueeze(2).to_broadcast([P, 32, NK, 2])

            def hot_y(m, hf):
                wait(dve, "lists_evac", m + 1)
                wait(dve, "hotlo_done", m * 2 - 1 + hf)
                dve.tensor_tensor(hoty[:, hot_slice(hf)], iota[:, 1].unsqueeze(1).to_broadcast([P, 32, NK, 2]),
                                  spread(1, hf), ALU.is_equal).then_inc(s["hoty_done"], 1)

            def hot_x(m, par, hf):
                wait(dve, "p_mm", m - 1)
                dve.tensor_tensor(hotx[:, par, hot_slice(hf)], iota[:, 0].unsqueeze(1).to_broadcast([P, 32, NK, 2]),
                                  spread(0, hf), ALU.is_equal)

            def hot_w(m, par, hf):
                wait(dve, "hoty_done", m * 2 + (hf + 1))
                dve.tensor_tensor(hotw[:, par, 0, hot_slice(hf)], hoty[:, hot_slice(hf)], spread(2, hf),
                                  ALU.mult).then_inc(s["hot_done"], 1)

            def step(m, hot_par, hot_before, finish_quad=None):
                for t in range(2):
                    hold(dve, "sims_ready", m * 2 + (t + 1))
                    for r in range(ROWS):
                        p, h = r // H, r % H
                        last = dve.max(vals[:, p, t * H + h, :], sims[:, t, r, :])
                    last.then_inc(s["vals_done"], 1)
                wait(dve, "code_done", m)
                for t in range(2):
                    hold(dve, "vals_done", m * 2 + (t + 1))
                    for r in range(ROWS):
                        p, h = r // H, r % H
                        last = dve.max_index(idx[:, p, t * H + h, :], vals[:, p, t * H + h, :], sims[:, t, r, :])
                    last.then_inc(s["idx_done"], 1)
                vx, vy = vals[:, 0], vals[:, 1]
                dve.tensor_tensor(cand[:, :, 0:8], vx[:, :, 0:1].to_broadcast([P, RH, 8]), vy, ALU.add)
                dve.tensor_tensor(cand[:, :, 8:12], vx[:, :, 1:2].to_broadcast([P, RH, 4]), vy[:, :, 0:4], ALU.add)
                dve.tensor_tensor(cand[:, :, 12:16].rearrange("p h (a b) -> p h a b", a=2),
                                  vx[:, :, 2:4].unsqueeze(3).to_broadcast([P, RH, 2, 2]),
                                  vy[:, :, 0:2].unsqueeze(2).to_broadcast([P, RH, 2, 2]), ALU.add)
                dve.tensor_tensor(cand[:, :, 16:20], vx[:, :, 4:8], vy[:, :, 0:1].to_broadcast([P, RH, 4]),
                                  ALU.add).then_inc(s["cand_done"], 1)
                if hot_before:
                    hot_y(m - 1, 0)
                    hot_x(m - 1, hot_par, 0)
                hold(dve, "cand_done", m + 1)
                for r in range(RH):
                    last = dve.max(top[:, r, :], cand[:, r, :])
                last.then_inc(s["top_done"], 1)
                wait(dve, "ex_done", m)
                wait(dve, "top_done", m + 1)
                dve.tensor_tensor(dif[:, :, :], cand[:, :, :], top[:, :, 0:1].to_broadcast([P, RH, NCAND]),
                                  ALU.subtract).then_inc(s["dif_done"], 1)
                if hot_before:
                    hot_w(m - 1, hot_par, 0)
                for r in range(RH):
                    last = dve.match_replace(marked[:, r, :], top[:, r, :], cand[:, r, :], REPLACED)
                last.then_inc(s["marked_done"], 1)
                if hot_before:
                    hot_y(m - 1, 1)
                wait(dve, "code_done", m + 1)
                wait(dve, "marked_done", m + 1)
                for w in range(2):
                    last = dve.scalar_tensor_tensor(
                        out=words16[:, w, :, 1],
                        in0=marked[:, :, :].rearrange("p h c -> p (h c)"), scalar=REPLACED / 2,
                        in1=code[:, :, :].rearrange("p h c -> p (h c)"),
                        op0=ALU.is_lt, op1=ALU.mult)
                last.then_inc(s["hi_done"], 1)
                if hot_before:
                    hot_x(m - 1, hot_par, 1)
                wait(dve, "lo_done", m + 1)
                hold(dve, "hi_done", m + 1)
                for w in range(2):
                    for r in range(RH):
                        last = dve.max(picked[:, w, r, :], words[:, w, r, :])
                last.then_inc(s["picked_done"], 1)
                if hot_before:
                    hot_w(m - 1, hot_par, 1)
                wait(dve, "conv_done", m)
                wait(dve, "picked_done", m + 1)
                dve.tensor_copy(exk16, picked16[:, :, :, 0]).then_inc(s["exk_done"], 1)
                dve.tensor_scalar(codes[:, 0, :], picked16[:, 0, :, 1], NK * (NK - 1), None, ALU.bitwise_and)
                wait(dve, "exk_done", m + 1)
                dve.reduce_sum(zsum[:, :], exk[:, :, :], AX_X).then_inc(s["z_done"], 1)
                dve.tensor_scalar(codes[:, 1, :], picked16[:, 0, :, 1], NK - 1, None,
                                  ALU.bitwise_and).then_inc(s["codes_done"], 1)
                wait(dve, "z_done", m + 1)
                dve.reciprocal(zinv[:, :], zsum[:, :]).then_inc(s["zinv_done"], 1)
                wait(dve, "zinv_done", m + 1)
                dve.scalar_tensor_tensor(out=wk[:, :, :], in0=exk[:, :, :], scalar=W_SCALE,
                                         in1=zinv[:, :].unsqueeze(2).to_broadcast([P, RH, TOPK]), op0=ALU.mult,
                                         op1=ALU.mult).then_inc(s["wk_done"], 1)
                wait(dve, "lists_mm", m)
                wait(dve, "wk_done", m + 1)
                flat = wk[:, :, :].rearrange("p h k -> p (h k)")
                dve.tensor_copy(lists[:, 2, :], flat).then_inc(s["whi_done"], 1)
                wait(dve, "whi_done", m + 1)
                dve.tensor_tensor(lists[:, 3, :], flat, lists[:, 2, :], ALU.subtract).then_inc(s["wlo_done"], 1)

            def residual(q):
                wait(dve, "out_done", q)
                wait(dve, "y2_mm", q + 1)
                dve.tensor_tensor(zf[:, :, :], b_y2.rearrange("p (t d) -> p t d", t=CH), x1[:, bass.ds(q * CH, CH), :],
                                  ALU.add).then_inc(s["zf_done"], 1)
                wait(dve, "zf_done", q + 1)
                for t in range(CH):
                    last = dve.bn_stats(st2[:, t, :], zf[:, t, :])
                last.then_inc(s["st2_done"], 1)
                hold(dve, "st2_done", q + 1)
                for t in range(CH):
                    last = dve.bn_aggr(mv2[:, t, :], st2[:, t, :])
                last.then_inc(s["mv2_done"], 1)

            def norm_out(q):
                wait(dve, "sd2", q + 1)
                dve.reciprocal(rstd2[:, :], rstd2[:, :]).then_inc(s["rstd2_done"], 1)
                wait(dve, "rstd2_done", q + 1)
                wait(dve, "stored", q * 16)
                for t in range(CH):
                    last = dve.tensor_scalar(outb[:, t, :], zf[:, t, :], mv2[:, t, 0:1], rstd2[:, t:t + 1],
                                             ALU.subtract, ALU.mult)
                last.then_inc(s["out_done"], 1)

            def quad(q, before, before2):
                step(q * 2, 1, before)
                if before2:
                    residual(q - 2)
                step(q * 2 + 1, 0, True)
                if before2:
                    norm_out(q - 2)

            quad(0, False, False)
            quad(1, True, False)
            quad(2, True, True)
            with dve.Fori(3, NCH) as q:
                quad(q, True, True)
            for hf in range(2):
                hot_y(T // 2 - 1, hf)
                hot_x(T // 2 - 1, 1, hf)
                hot_w(T // 2 - 1, 1, hf)
            residual(NCH - 2)
            norm_out(NCH - 2)
            residual(NCH - 1)
            norm_out(NCH - 1)

        @block.tensor
        def _(pe):
            def weights(g):
                if g >= 2:
                    pe.wait_ge(s["w_evac"], g - 1)
                lo, hi = W_GROUPS[g]
                for n in range(lo, hi):
                    last = pe.transpose(b_w[g][:, (n - lo) * P:(n - lo + 1) * P], nat[:, n, :], ident[:, :])
                last.then_inc(s["w_trn"], 1)

            def turn_x(g, k):
                wait(pe, f"ld_x{k}", g * 16 + 16)
                wait(pe, "xT_evac", g * GR + k)
                for t in range(CH):
                    last = pe.transpose(b_xT[:, t * P:(t + 1) * P], xs[:, k, t, :], ident[:, :])
                last.then_inc(s["xT_mm"], 1)

            def project(g, k):
                c = g * GR + k
                wait(pe, "xT_evac", c + 1)
                for n, (to, done, used, uses) in enumerate((
                        (b_delta[k % 2], "z_delta", "relu_done", c - 1), (b_in, "z_in", "tin_done", c),
                        (b_sel, "z_sel", "sel_done", c), (b_gate, "z_gate", "gate_done", c))):
                    wait(pe, used, uses)
                    pe.matmul(to, trn[:, n, :], xT[:, k], start=True, stop=True).then_inc(s[done], 1)

            def project_out(g, k):
                c = g * GR + k
                wait(pe, "gated", c + 1)
                wait(pe, "x1_sum", c)
                for t in range(CH):
                    last = pe.matmul(b_y1[:, t * P:(t + 1) * P], outg[:, k, t * P:(t + 1) * P], trn[:, 4, :],
                                     start=True, stop=True)
                last.then_inc(s["y1_mm"], 1)

            def projections(g):
                for k in range(GR):
                    if k + 1 < GR:
                        turn_x(g, k + 1)
                    project(g, k)

            pe.wait_ge(s["c_ident"], 2)
            pe.wait_ge(s["ld_w"], 64)
            weights(0)
            turn_x(0, 0)
            pe.wait_ge(s["ld_wout"], 16)
            weights(1)
            pe.wait_ge(s["w_evac"], 1)
            projections(0)
            with pe.Fori(1, NG) as g:
                turn_x(g, 0)
                projections(g)
                for k in range(GR):
                    project_out(g - 1, k)
            pe.wait_ge(s["ld_keys"], 16 * 11)
            for g in range(2, 5):
                weights(g)
            for k in range(GR):
                project_out(NG - 1, k)
            pe.wait_ge(s["w_evac"], 5)
            for r in range(ROWS):
                p, h = r // H, r % H
                last = pe.matmul(b_m[:, r * NK:(r + 1) * NK], wq[:, r, :],
                                 trn[:, 5 + 2 * (h // 4) + p, (h % 4) * NK:(h % 4 + 1) * NK], start=True, stop=True)
            last.then_inc(s["m_mm"], 1)

            def turn_x1(g):
                for k in range(GR):
                    wait(pe, "nrm", g * GR + (k + 1))
                    wait(pe, "bst_done", g * GR + (k + 1 - GR))
                    for t in range(CH):
                        last = pe.transpose(b_x1T[k][:, t * P:(t + 1) * P], xs[:, k, t, :], ident[:, :])
                    last.then_inc(s["x1T_mm"], 1)

            turn_x1(0)
            with pe.Fori(1, NG) as g:
                turn_x1(g)
            pe.wait_ge(s["m_evac"], 1)
            pe.wait_ge(s["x1T_evac"], NCH)

            def scores(m):
                for t in range(2):
                    wait(pe, "xn_done", m * 2 + (t + 1))
                    wait(pe, "sims_ready", m * 2 - 1 + t)
                    pe.matmul(b_sim[t], xn[:, t], msim[:, :], start=True, stop=True).then_inc(s["sim_mm"], 1)

            def lists_turned(m):
                wait(pe, "conv_done", m + 1)
                wait(pe, "wlo_done", m + 1)
                wait(pe, "lists_evac", m)
                for f in range(4):
                    last = pe.transpose(b_lists[:, f * P:(f + 1) * P], lists[:, f, :], ident16[:, :])
                last.then_inc(s["lists_mm"], 1)

            def scatter(m, par):
                hold(pe, "p_evac", m * 2)
                for hf in range(2):
                    wait(pe, "hot_done", m * 2 + (hf + 1))
                    hold(pe, "hotlo_done", m * 2 + (hf + 1))
                    for g in range(32):
                        for c in (2 * hf, 2 * hf + 1):
                            tok = 32 * c + g
                            for tile in range(2):
                                rows = slice(64 * tile, 64 * tile + 64)
                                at = 1024 * tile + NK * g
                                for part in range(2):
                                    last = pe.matmul(psum[32 * c:32 * c + 32, at:at + NK],
                                                     hotx[rows, par, tok // 2, :, tok % 2],
                                                     hotw[rows, par, part, tok // 2, :, tok % 2],
                                                     start=(part == 0), stop=(part == 1))
                last.then_inc(s["p_mm"], 1)

            def experts_in(q):
                wait(pe, "p_evac", q * 4 + 4)
                for jh in range(JH):
                    if jh >= 4:
                        wait(pe, "gelu_done", q * JH + (jh - 3))
                    pe.matmul(b_g[jh % 4], trn[:, 9 + jh, :],
                              x1T[:, bass.ds(q * CW, CW)], start=True, stop=True).then_inc(s["g_mm"], 1)

            def experts_out(q):
                wait(pe, "a_done", q * JH + JH)
                wait(pe, "zf_done", q)
                for t in range(CH):
                    for jh in range(JH):
                        last = pe.matmul(b_y2[:, t * P:(t + 1) * P],
                                         gl[:, jh, t * P:(t + 1) * P], ko[:, jh, :], start=(jh == 0), stop=(jh == JH - 1))
                last.then_inc(s["y2_mm"], 1)

            def quad(q, before, before2):
                if before:
                    lists_turned(q * 2 - 1)
                scores(q * 2 + 1)
                if before2:
                    experts_out(q - 2)
                if before:
                    scatter(q * 2 - 1, 1)
                lists_turned(q * 2)
                scores(q * 2 + 2)
                if before:
                    experts_in(q - 1)
                    wait(pe, "gelu_done", (q - 1) * JH + JH)
                scatter(q * 2, 0)

            scores(0)
            quad(0, False, False)
            quad(1, True, False)
            quad(2, True, True)
            with pe.Fori(3, NCH) as q:
                quad(q, True, True)
            lists_turned(T // 2 - 1)
            experts_out(NCH - 2)
            scatter(T // 2 - 1, 1)
            experts_in(NCH - 1)
            experts_out(NCH - 1)


_INS = ['L0_attn_x', 'L0_attn_W_in', 'L0_attn_W_select', 'L0_attn_W_gate', 'L0_attn_W_out', 'L0_attn_W_delta',
        'L0_attn_log_a', 'L0_ffn_gamma', 'L0_ffn_beta', 'L0_ffn_w_q', 'L0_ffn_keys', 'L0_ffn_key_in',
        'L0_ffn_key_out']


def kernel(**inputs):
    import numpy as _np
    import concourse.bacc as _bacc
    from concourse import mybir as _mybir
    from concourse.bass_utils import run_bass_kernel_spmd as _run

    nc = _bacc.Bacc("TRN2", target_bir_lowering=False, num_devices=1)
    arrays, args = {}, []
    for name in _INS:
        a = _np.ascontiguousarray(inputs[name])
        arrays[f"in_{name}_dram"] = a
        args.append(nc.dram_tensor(f"in_{name}_dram", a.shape, _mybir.dt.from_np(a.dtype), kind="ExternalInput").ap())
    shape = inputs['L0_attn_x'].shape
    args.append(nc.dram_tensor("out_0_dram", shape, _mybir.dt.float32, kind="ExternalOutput").ap())
    seqffn_kernel(nc, *args)
    r = _run(nc, [arrays], core_ids=[0])
    return r.results[0]["out_0_dram"]
```

```python
from contextlib import ExitStack

import concourse.bass as bass
from concourse import mybir

ALU = mybir.AluOpType
ACT = mybir.ActivationFunctionType
AX_X = mybir.AxisListType.X
F32 = mybir.dt.float32
F16 = mybir.dt.float16
U16 = mybir.dt.uint16
U32 = mybir.dt.uint32
I32 = mybir.dt.int32

P = 128
LN_EPS = 1e-5
BN_EPS = 1e-5
W_SCALE = 2.0 ** 14
REPLACED = -3.0e38
CODE_BASE = 128


def seqffn_kernel(nc, x, w_in, w_select, w_gate, w_out, w_delta, log_a, gamma, beta, w_q, keys,
                  key_in, key_out, out):
    B, S, D = x.shape
    H, NK, _, KD = keys.shape
    NE = NK * NK
    TOPK = 8
    T = B * S // P
    CH = 4
    CW = CH * P
    NCH = T // CH
    GR = 4
    NG = NCH // GR
    ROW_CH = S // CW
    ROWS = 2 * H
    NCAND = 20
    SL = H * TOPK
    JL, JH = 4, NK // 4
    assert D == P and KD == P and NK == 32 and H == 8 and NE == JH * P and GR % ROW_CH == 0

    x_v = x.rearrange("b (n p) d -> p (b n) d", p=P)
    out_v = out.rearrange("b (n p) d -> p (b n) d", p=P)

    with ExitStack() as ctx:
        def sb(name, shape, dt=F32):
            return ctx.enter_context(nc.sbuf_tensor(name, shape, dt))

        def sem(name):
            return ctx.enter_context(nc.semaphore(name))

        psum = ctx.enter_context(nc.psum_tensor("psum", [P, 8 * 512], F32))

        def bank(i):
            return psum[:, i * 512:(i + 1) * 512]

        ident = sb("ident", [P, P])
        ident16 = sb("ident16", [P, P], F16)
        iota_i = sb("iota_i", [P, 2, NK, 2], I32)
        iota = sb("iota", [P, 2, NK, 2], F16)
        eps = sb("eps", [P, 1])
        cols = sb("cols", [P, 3])
        a_base = sb("a_base", [P, 1])
        neg_a = sb("neg_a", [P, 1])
        nat = sb("nat", [P, 17, P])
        trn = sb("trn", [P, 17, P])
        ko = sb("ko", [P, JH, P])
        msim = sb("msim", [P, ROWS * NK])
        stage = sb("stage", [P, (GR * CH + ROWS) * P])
        xs = stage[:, 0:GR * CW].rearrange("p (k t d) -> p k t d", k=GR, t=CH)
        wq = stage[:, GR * CW:].rearrange("p (r d) -> p r d", r=ROWS)
        arena = sb("arena", [P, 27648])
        xT, absd, ex1, lnd, relu, sp, decay, tin, sel, gate, states, outg = (
            arena[:, i * GR * CW:(i + 1) * GR * CW].rearrange("p (k w) -> p k w", k=GR) for i in range(12))
        st1 = sb("st1", [P, T, 6])
        mv1 = sb("mv1", [P, T, 2])
        rstd1 = sb("rstd1", [P, T])
        x1 = sb("x1", [P, T, P])
        x1T = sb("x1T", [P, T * P])
        bst = sb("bst", [P, NCH, 6])
        bmv = sb("bmv", [P, 2])
        bsd = sb("bsd", [P, 1])
        bsc = sb("bsc", [P, 2])
        RH = 2 * H
        xn = sb("xn", [P, 2, P])
        sims = sb("sims", [P, 2, ROWS, NK])
        vals = sb("vals", [P, 2, RH, TOPK])
        idx = sb("idx", [P, 2, RH, TOPK], U32)
        ixf = sb("ixf", [P, RH, TOPK])
        iyf = sb("iyf", [P, RH, TOPK])
        cand = sb("cand", [P, RH, NCAND])
        code = sb("code", [P, RH, NCAND])
        top = sb("top", [P, RH, TOPK])
        dif = sb("dif", [P, RH, NCAND])
        ex = sb("ex", [P, RH * NCAND])
        marked = sb("marked", [P, RH, NCAND])
        words = sb("words", [P, 2, RH, NCAND])
        picked = sb("picked", [P, 2, RH, TOPK])
        exk = sb("exk", [P, RH, TOPK])
        zsum = sb("zsum", [P, RH])
        zinv = sb("zinv", [P, RH])
        wk = sb("wk", [P, RH, TOPK])
        codes = sb("codes", [P, 2, 2 * SL], U16)
        lists = sb("lists", [P, 4, 2 * SL], F16)
        listsT = sb("listsT", [P, 4, P], F16)
        HW = P // 2 * NK
        assert stage.shape[1] == NK * P
        pev = tuple(x.rearrange("p (j t) -> p j t", j=NK) for x in (arena[:, 0:NK * P], stage[:, :]))
        gl = arena[:, 4096:8192].rearrange("p (j w) -> p j w", j=JH)
        pt = arena[:, 8192:12288].rearrange("p (j w) -> p j w", j=JH)
        gl_last = arena[:, 12288 + 3 * HW:12288 + 5 * HW].rearrange("p (j w) -> p j w", j=JH)
        hots = arena[:, 12288:12288 + 7 * HW].bitcast(F16)
        hoty = hots[:, 0:2 * HW].rearrange("p (t k s) -> p t k s", k=NK, s=2)
        hotx = hots[:, 2 * HW:6 * HW].rearrange("p (b t k s) -> p b t k s", b=2, k=NK, s=2)
        hotw = hots[:, 6 * HW:14 * HW].rearrange("p (b w t k s) -> p b w t k s", b=2, w=2, k=NK, s=2)
        zf = nat[:, 0:CH, :]
        st2 = sb("st2", [P, CH, 6])
        mv2 = sb("mv2", [P, CH, 2])
        rstd2 = sb("rstd2", [P, CH])
        nmr2 = sb("nmr2", [P, CH])
        outb = nat[:, CH:2 * CH, :]

        words16 = words[:, :, :, :].rearrange("p w h c -> p w (h c)").bitcast(U16).rearrange(
            "p w (c s) -> p w c s", s=2)
        picked16 = picked[:, :, :, :].rearrange("p w h k -> p w (h k)").bitcast(U16).rearrange(
            "p w (k s) -> p w k s", s=2)
        ex16 = ex[:, :].bitcast(U16).rearrange("p (c s) -> p s c", s=2)
        exk16 = exk[:, :, :].rearrange("p h k -> p (h k)").bitcast(U16).rearrange(
            "p (k s) -> p s k", s=2)
        b_xT, b_delta, b_in, b_sel, b_gate = bank(0), (bank(1), bank(2)), bank(3), bank(4), bank(5)
        b_y1 = (bank(6), bank(7))
        b_w, b_m = (bank(7), bank(6), bank(0), bank(1), bank(2)), bank(0)
        b_x1T = tuple(bank(1 + i) for i in range(GR))
        b_sim, b_y2 = (bank(4), bank(5)), bank(6)
        b_g = (bank(6), bank(7))
        b_lists = bank(7)[:, 0:256].bitcast(F16)

        names = """passed iota_done ld_w ld_wout ld_keys ld_rest ld_x ld_x0 ld_x1 ld_x2 ld_x3 c_ident c_iota c_misc
            w_trn w_evac m_mm m_evac c_cols c_nega
            xT_mm xT_evac z_delta z_in z_sel z_gate abs_done relu_done e_done ln_done sp_raw sp_done decay_done
            tin_done sel_done gate_done upd_done scan_done gated y1_mm x1_sum st1_done mv1_done sd1 rstd1_done
            nrm x1T_mm x1T_evac bst_done x1_copy bmv_done bsd_done bsd_inv bsc_half bsc_mu bsc_done
            xn_done sim_mm sims_ready vals_done idx_done ixf_done cand_done top_done dif_done ex_done
            lo_done code_done marked_done hi_done hi2_done picked_done exk_done codes_done z_done zinv_done
            wk_done whi_done wlo_done conv_done lists_mm lists_evac hoty_done hot_done hotlo_done
            p_mm p_evac relaid g_mm gelu_done a_done a_last tile_done y2_mm zf_done st2_done mv2_done sd2 rstd2_done nmr2_done
            out_done stored""".split()
        s = {n: sem(n) for n in names}

        HALF, REST = range(JH // 2), range(JH // 2, JH)

        W_GROUPS = ((0, 4), (4, 5), (5, 9), (9, 13), (13, 17))

        block = ctx.enter_context(nc.Block())

        def wait(eng, name, value):
            if isinstance(value, int) and value <= 0:
                return
            eng.wait_ge(s[name], value)

        def hold(eng, name, value):
            wait(eng, name, value)
            if not isinstance(value, int):
                eng.sem_inc(s["passed"], 1)

        @block.sync
        def _(sp_eng):
            def group(g):
                for k in range(GR):
                    wait(sp_eng, "xT_mm", g * GR + (k + 1 - GR))
                    sp_eng.dma_start(xs[:, k, :, :], x_v[:, bass.ds(g * (GR * CH) + k * CH, CH), :]).then_inc(
                        s[f"ld_x{k}"], 16)
                    if g == 0 and k == 0:
                        for n, w in enumerate((w_delta, w_in, w_select, w_gate)):
                            sp_eng.dma_start(nat[:, n, :], w).then_inc(s["ld_w"], 16)

            group(0)
            for k in range(B):
                n = T // B
                sp_eng.dma_start(x1[:, k * n:(k + 1) * n, :], x_v[:, k * n:(k + 1) * n, :]).then_inc(s["ld_x"], 16)
            for g in range(1, NG):
                group(g)
            for g in range(2):
                sp_eng.dma_start(nat[:, 5 + 2 * g:7 + 2 * g, :],
                                 keys[4 * g:4 * g + 4].rearrange("h k p d -> (h k) p d")).then_inc(s["ld_keys"], 16)
            for jl in range(JL):
                for dst, src in ((nat[32 * jl:32 * jl + 32, 9:17, :], key_in), (ko[32 * jl:32 * jl + 32, :, :], key_out)):
                    sp_eng.dma_start(dst, src.rearrange("(i l h) d -> l i h d", l=JL, h=JH)[jl]).then_inc(s["ld_keys"], 16)
            sp_eng.dma_start(wq[:, :, :], w_q.rearrange("(r k) d -> k r d", k=P)).then_inc(s["ld_keys"], 16)

            last = NCH - 1

            def relayout(q):
                hold(sp_eng, "p_evac", q * 8 + 8)
                if q is last:
                    sp_eng.wait_ge(s["a_last"], JH)
                else:
                    wait(sp_eng, "a_done", q * JH)
                for b in range(2):
                    for e in range(2):
                        c, rows = 2 * b + e, slice(64 * e + 32 * b, 64 * e + 32 * b + 32)
                        for jl in range(JL):
                            sp_eng.dma_start(pt[32 * jl:32 * jl + 32, :, c * P:(c + 1) * P],
                                             pev[b][rows, jl * JH:(jl + 1) * JH, :]).then_inc(s["relaid"], 16)

            def store(q):
                wait(sp_eng, "out_done", q + 1)
                sp_eng.dma_start(out_v[:, bass.ds(q * CH, CH), :], outb[:, :, :]).then_inc(s["stored"], 16)

            relayout(0)
            with sp_eng.Fori(1, last - 1) as q:
                relayout(q)
                store(q - 1)
            relayout(last - 1)
            relayout(last)
            for q in range(last - 2, NCH):
                store(q)
            sp_eng.wait_ge(s["stored"], 16 * NCH)

        @block.gpsimd
        def _(pool):
            pool.memset(ident[:, :], 0.0)
            pool.memset(ident16[:, :], 0.0)
            pool.memset(eps[:, :], LN_EPS).then_inc(s["c_misc"], 1)
            pool.wait_ge(s["c_misc"], 1)
            for m in (ident, ident16):
                pool.affine_select(out=m[:, :], in_=m[:, :], compare_op=ALU.not_equal, fill=1.0, base=0,
                                   pattern=[[-1, P]], channel_multiplier=1).then_inc(s["c_ident"], 1)
            pool.iota(iota_i[:, 0], pattern=[[NK, NK], [0, 2]], base=0, channel_multiplier=0)
            pool.iota(iota_i[:, 1], pattern=[[1, NK], [0, 2]], base=0, channel_multiplier=0).then_inc(s["c_iota"], 1)
            def update(g, k):
                c = g * GR + k
                wait(pool, "tin_done", c + 1)
                wait(pool, "sel_done", c + 1)
                pool.tensor_tensor(tin[:, k], tin[:, k], sel[:, k], ALU.mult).then_inc(s["upd_done"], 1)

            def gate_out(g, k):
                c = g * GR + k
                wait(pool, "scan_done", c + 1)
                wait(pool, "gate_done", c + 1)
                wait(pool, "y1_mm", c + 1 - GR)
                pool.tensor_tensor(outg[:, k], states[:, k], gate[:, k], ALU.mult).then_inc(s["gated"], 1)

            for g in range(NG):
                for k in range(GR if g else 0):
                    gate_out(g - 1, k)
                for k in range(GR):
                    update(g, k)
            for k in range(GR):
                gate_out(NG - 1, k)

            def x1_back(g):
                for k in range(GR):
                    wait(pool, "nrm", g * GR + (k + 1))
                    pool.tensor_copy(x1[:, bass.ds(g * (GR * CH) + k * CH, CH), :], xs[:, k, :, :]).then_inc(s["x1_copy"], 1)

            x1_back(0)
            with pool.Fori(1, NG) as g:
                x1_back(g)
            def low_part(m, par, hf):
                g = slice(32 * hf, 32 * hf + 32)
                wait(pool, "hoty_done", m * 2 + (hf + 1))
                wait(pool, "p_mm", m * 2 - 3 + hf)
                w_lo = listsT[:, 3, 64 * hf:64 * hf + 64].rearrange("p (g s) -> p g s", s=2)
                pool.tensor_tensor(
                    hotw[:, par, 1, g, :, :], hoty[:, g, :, :],
                    w_lo.unsqueeze(2).to_broadcast([P, 32, NK, 2]), ALU.mult).then_inc(s["hotlo_done"], 1)

            def candidate_sums(m):
                wait(pool, "vals_done", m * 2 + 2)
                wait(pool, "marked_done", m)
                vx, vy = vals[:, 0], vals[:, 1]
                pool.tensor_tensor(cand[:, :, 0:8], vx[:, :, 0:1].to_broadcast([P, RH, 8]), vy, ALU.add)
                pool.tensor_tensor(cand[:, :, 8:12], vx[:, :, 1:2].to_broadcast([P, RH, 4]), vy[:, :, 0:4], ALU.add)
                pool.tensor_tensor(cand[:, :, 12:16].rearrange("p h (a b) -> p h a b", a=2),
                                   vx[:, :, 2:4].unsqueeze(3).to_broadcast([P, RH, 2, 2]),
                                   vy[:, :, 0:2].unsqueeze(2).to_broadcast([P, RH, 2, 2]), ALU.add)
                pool.tensor_tensor(cand[:, :, 16:20], vx[:, :, 4:8], vy[:, :, 0:1].to_broadcast([P, RH, 4]),
                                   ALU.add).then_inc(s["cand_done"], 1)
                wait(pool, "cand_done", m + 1)
                wait(pool, "ex_done", m)
                pool.tensor_tensor(dif[:, :, :], cand[:, :, :], cand[:, :, 0:1].to_broadcast([P, RH, NCAND]),
                                   ALU.subtract).then_inc(s["dif_done"], 1)

            def high_halves(m):
                hold(pool, "hi_done", m + 1)
                pool.tensor_copy(words16[:, 1, :, 1], words16[:, 0, :, 1]).then_inc(s["hi2_done"], 1)

            def halves(m):
                wait(pool, "lists_mm", m)
                hold(pool, "wk_done", m + 1)
                flat = wk[:, :, :].rearrange("p h k -> p (h k)")
                pool.tensor_copy(lists[:, 2, :], flat).then_inc(s["whi_done"], 1)
                wait(pool, "whi_done", m + 1)
                pool.tensor_tensor(lists[:, 3, :], flat, lists[:, 2, :], ALU.subtract).then_inc(s["wlo_done"], 1)

            def candidate_codes(m):
                hold(pool, "idx_done", m * 2 + 2)
                pool.tensor_copy(iyf[:, :, :], idx[:, 1])
                pool.tensor_scalar(ixf[:, :, :], idx[:, 0], float(CODE_BASE), float(NK), ALU.add, ALU.mult).then_inc(
                    s["ixf_done"], 1)
                wait(pool, "ixf_done", m + 1)
                wait(pool, "hi_done", m)
                iy = iyf[:, :, :]
                pool.tensor_tensor(code[:, :, 0:8], ixf[:, :, 0:1].to_broadcast([P, RH, 8]), iy, ALU.add)
                pool.tensor_tensor(code[:, :, 8:12], ixf[:, :, 1:2].to_broadcast([P, RH, 4]), iy[:, :, 0:4], ALU.add)
                pool.tensor_tensor(code[:, :, 12:16].rearrange("p h (a b) -> p h a b", a=2),
                                   ixf[:, :, 2:4].unsqueeze(3).to_broadcast([P, RH, 2, 2]),
                                   iy[:, :, 0:2].unsqueeze(2).to_broadcast([P, RH, 2, 2]), ALU.add)
                pool.tensor_tensor(code[:, :, 16:20], ixf[:, :, 4:8], iy[:, :, 0:1].to_broadcast([P, RH, 4]),
                                   ALU.add).then_inc(s["code_done"], 1)

            def weigh(q, jhs):
                wait(pool, "relaid", q * 256 + 256)
                for jh in jhs:
                    wait(pool, "gelu_done", q * JH + (jh + 1))
                    by_token = gl[:, jh].rearrange("p (n c) -> p n c", c=4)
                    pool.tensor_tensor(by_token, pt[:, jh].rearrange("p (c n) -> p n c", c=4), by_token,
                                       ALU.mult).then_inc(s["a_done"], 1)

            def quad(q, before, before2):
                candidate_sums(q * 2)
                candidate_codes(q * 2)
                if before:
                    low_part(q * 2 - 1, 1, 0)
                    low_part(q * 2 - 1, 1, 1)
                high_halves(q * 2)
                if before2:
                    weigh(q - 2, HALF)
                halves(q * 2)
                if before2:
                    weigh(q - 2, REST)
                candidate_sums(q * 2 + 1)
                candidate_codes(q * 2 + 1)
                low_part(q * 2, 0, 0)
                low_part(q * 2, 0, 1)
                high_halves(q * 2 + 1)
                halves(q * 2 + 1)

            quad(0, False, False)
            quad(1, True, False)
            with pool.Fori(2, NCH) as q:
                quad(q, True, True)
            low_part(T // 2 - 1, 1, 0)
            low_part(T // 2 - 1, 1, 1)

        @block.scalar
        def _(act):
            act.dma_start(cols[:, 0:1], log_a.rearrange("(d o) -> d o", o=1)).then_inc(s["ld_rest"], 16)
            act.dma_start(cols[:, 1:2], gamma.rearrange("(d o) -> d o", o=1)).then_inc(s["ld_rest"], 16)
            act.dma_start(cols[:, 2:3], beta.rearrange("(d o) -> d o", o=1)).then_inc(s["ld_rest"], 16)
            act.dma_start(nat[:, 4, :], w_out).then_inc(s["ld_wout"], 16)

            def weights_out(g):
                lo, hi = W_GROUPS[g]
                act.wait_ge(s["w_trn"], g + 1)
                act.activation(trn[:, lo:hi, :], b_w[g][:, 0:(hi - lo) * P], ACT.Copy).then_inc(s["w_evac"], 1)

            weights_out(0)
            act.wait_ge(s["ld_rest"], 48)
            act.activation(a_base[:, :], cols[:, 0:1], ACT.Sigmoid).then_inc(s["c_cols"], 1)
            act.wait_ge(s["c_cols"], 1)
            act.mul(neg_a[:, :], a_base[:, :], -1.0).then_inc(s["c_nega"], 1)

            def group(g):
                for k in range(GR):
                    c = g * GR + k
                    wait(act, "z_delta", c + 1)
                    wait(act, "e_done", c + 1 - GR)
                    act.activation(absd[:, k], b_delta[k % 2], ACT.Abs).then_inc(s["abs_done"], 1)
                    wait(act, "z_in", c + 1)
                    wait(act, "scan_done", c + 1 - GR)
                    act.activation(tin[:, k], b_in, ACT.Tanh).then_inc(s["tin_done"], 1)
                    wait(act, "abs_done", c + 1)
                    wait(act, "ln_done", c + 1 - GR)
                    act.activation(ex1[:, k], absd[:, k], ACT.Exp, scale=-1.0).then_inc(s["e_done"], 1)
                for k in range(GR):
                    c = g * GR + k
                    wait(act, "e_done", c + 1)
                    wait(act, "sp_raw", c + 1 - GR)
                    act.activation(lnd[:, k], ex1[:, k], ACT.Ln, bias=1.0).then_inc(s["ln_done"], 1)
                if g == 0:
                    weights_out(1)
                for k in range(GR):
                    c = g * GR + k
                    wait(act, "z_sel", c + 1)
                    wait(act, "upd_done", c + 1 - GR)
                    act.activation(sel[:, k], b_sel, ACT.Sigmoid).then_inc(s["sel_done"], 1)
                    wait(act, "z_gate", c + 1)
                    wait(act, "gated", c + 1 - GR)
                    act.activation(gate[:, k], b_gate, ACT.Sigmoid).then_inc(s["gate_done"], 1)
                for k in range(GR):
                    c = g * GR + k
                    wait(act, "sp_done", c + 1)
                    wait(act, "scan_done", c + 1 - GR)
                    act.activation(decay[:, k], sp[:, k], ACT.Exp, scale=neg_a[:, 0:1]).then_inc(s["decay_done"], 1)

            act.wait_ge(s["c_nega"], 1)
            for g in range(NG):
                group(g)
            for g in range(2, 5):
                weights_out(g)
            act.wait_ge(s["mv1_done"], 6)
            act.wait_ge(s["c_misc"], 1)
            act.activation(rstd1[:, :], mv1[:, :, 1], ACT.Sqrt, bias=eps[:, 0:1]).then_inc(s["sd1"], 1)
            act.wait_ge(s["m_mm"], 1)
            act.activation(msim[:, :], b_m, ACT.Copy).then_inc(s["m_evac"], 1)

            def x1T_out(g):
                for k in range(GR):
                    wait(act, "x1T_mm", g * GR + (k + 1))
                    act.activation(x1T[:, bass.ds(g * (GR * CW) + k * CW, CW)], b_x1T[k], ACT.Copy).then_inc(
                        s["x1T_evac"], 1)

            x1T_out(0)
            with act.Fori(1, NG) as g:
                x1T_out(g)
            act.wait_ge(s["bmv_done"], 1)
            act.activation(bsd[:, :], bmv[:, 1:2], ACT.Sqrt, bias=eps[:, 0:1]).then_inc(s["bsd_done"], 1)
            act.wait_ge(s["bsc_done"], 1)
            act.wait_ge(s["x1T_evac"], NCH)

            def normed(m):
                wait(act, "sim_mm", m * 2)
                for t in range(2):
                    last = act.activation(xn[:, t], x1T[:, bass.ds(m * (2 * P) + t * P, P)], ACT.Identity,
                                          bias=bsc[:, 1:2], scale=bsc[:, 0:1])
                    last.then_inc(s["xn_done"], 1)

            def sims_out(m):
                for t in range(2):
                    wait(act, "sim_mm", m * 2 + (t + 1))
                    wait(act, "idx_done", m * 2 - 1 + t)
                    act.activation(sims[:, t].rearrange("p r k -> p (r k)"), b_sim[t], ACT.Copy).then_inc(
                        s["sims_ready"], 1)

            def exps(m):
                wait(act, "dif_done", m + 1)
                wait(act, "lo_done", m)
                act.activation(ex[:, :], dif[:, :, :].rearrange("p h c -> p (h c)"), ACT.Exp).then_inc(s["ex_done"], 1)
                wait(act, "ex_done", m + 1)
                wait(act, "picked_done", m)
                act.activation(words16[:, :, :, 0], ex16, ACT.Copy).then_inc(s["lo_done"], 1)

            def convert(m):
                wait(act, "codes_done", m + 1)
                wait(act, "lists_mm", m)
                act.activation(lists[:, 0:2, :], codes[:, :, :], ACT.Copy).then_inc(s["conv_done"], 1)

            def lists_out(m):
                wait(act, "lists_mm", m + 1)
                wait(act, "hot_done", m * 2)
                wait(act, "hotlo_done", m * 2)
                act.activation(listsT[:, :, :].rearrange("p f t -> p (f t)"), b_lists, ACT.Copy).then_inc(s["lists_evac"], 1)

            def p_out(q, pair, hf):
                wait(act, "p_mm", q * 4 + (2 * pair + hf + 1))
                if pair == 0 and hf == 0:
                    wait(act, "relaid", q * 256)
                for b in range(2):
                    src = psum[:, 0:2048].rearrange("p (t k b j) -> p b j t k", t=2, b=2, j=NK)[:, b]
                    dst = pev[b].rearrange("p j (t h k) -> p j t h k", t=CH, h=2)[:, :, 2 * pair:2 * pair + 2, hf]
                    act.activation(dst, src, ACT.Copy, scale=1.0 / W_SCALE).then_inc(s["p_evac"], 1)

            def gelus(q, banks=b_g, to=gl, jhs=range(JH)):
                if to is gl:
                    wait(act, "y2_mm", q)
                for jh in jhs:
                    wait(act, "g_mm", q * JH + (jh + 1))
                    act.activation(to[:, jh], banks[jh % len(banks)], ACT.Gelu).then_inc(s["gelu_done"], 1)

            def spread2(q):
                wait(act, "mv2_done", q + 1)
                wait(act, "nmr2_done", q)
                wait(act, "out_done", q)
                act.activation(rstd2[:, :], mv2[:, :, 1], ACT.Sqrt, bias=eps[:, 0:1]).then_inc(s["sd2"], 1)

            def norm_out(q):
                wait(act, "nmr2_done", q + 1)
                wait(act, "stored", q * 16)
                for t in range(CH):
                    last = act.activation(outb[:, t, :], zf[:, t, :], ACT.Identity, bias=nmr2[:, t:t + 1],
                                          scale=rstd2[:, t:t + 1])
                last.then_inc(s["out_done"], 1)

            def quad(q, before, before2, last=False):
                if before:
                    lists_out(q * 2 - 1)
                    p_out(q - 1, 0, 1)
                if before2:
                    gelus(q - 2)
                exps(q * 2)
                if before:
                    p_out(q - 1, 1, 0)
                sims_out(q * 2 + 1)
                if not last:
                    normed(q * 2 + 2)
                convert(q * 2)
                lists_out(q * 2)
                if before:
                    p_out(q - 1, 1, 1)
                exps(q * 2 + 1)
                if not last:
                    sims_out(q * 2 + 2)
                    normed(q * 2 + 3)
                p_out(q, 0, 0)
                if before2 and not last:
                    spread2(q - 2)
                    norm_out(q - 2)
                convert(q * 2 + 1)

            normed(0)
            sims_out(0)
            normed(1)
            quad(0, False, False)
            quad(1, True, False)
            quad(2, True, True)
            with act.Fori(3, NCH - 1) as q:
                quad(q, True, True)
            quad(NCH - 1, True, True, last=True)
            gelus(NCH - 2, b_sim, jhs=HALF)
            lists_out(T // 2 - 1)
            p_out(NCH - 1, 0, 1)
            gelus(NCH - 2, b_sim, jhs=REST)
            p_out(NCH - 1, 1, 0)
            gelus(NCH - 1, b_sim, gl_last, HALF)
            p_out(NCH - 1, 1, 1)
            gelus(NCH - 1, b_sim, gl_last, REST)
            spread2(NCH - 3)
            norm_out(NCH - 3)
            spread2(NCH - 2)
            norm_out(NCH - 2)
            spread2(NCH - 1)
            norm_out(NCH - 1)

        @block.vector
        def _(dve):
            dve.wait_ge(s["c_iota"], 1)
            dve.tensor_copy(iota[:, :, :, :], iota_i[:, :, :, :]).then_inc(s["iota_done"], 1)

            def evac_x(g, k):
                c = g * GR + k
                wait(dve, "xT_mm", c + 1)
                wait(dve, "z_gate", c + 1 - GR)
                dve.tensor_copy(xT[:, k], b_xT).then_inc(s["xT_evac"], 1)

            def positive_part(g, k):
                c = g * GR + k
                wait(dve, "abs_done", c + 1)
                wait(dve, "sp_raw", c + 1 - GR)
                dve.tensor_scalar(relu[:, k], b_delta[k % 2], 0.0, None, ALU.max).then_inc(s["relu_done"], 1)

            def softplus(g, k):
                c = g * GR + k
                wait(dve, "ln_done", c + 1)
                wait(dve, "relu_done", c + 1)
                wait(dve, "decay_done", c + 1 - GR)
                dve.tensor_tensor(sp[:, k], relu[:, k], lnd[:, k], ALU.add).then_inc(s["sp_raw"], 1)
                wait(dve, "sp_raw", c + 1)
                dve.tensor_scalar(sp[:, k], sp[:, k], 1e-4, None, ALU.max).then_inc(s["sp_done"], 1)

            def scan(g, k):
                c = g * GR + k
                wait(dve, "upd_done", c + 1)
                wait(dve, "decay_done", c + 1)
                wait(dve, "gated", c + 1 - GR)
                wait(dve, "scan_done", c)
                dve.tensor_tensor_scan(states[:, k], decay[:, k], tin[:, k],
                                       0.0 if k % ROW_CH == 0 else states[:, k - 1, CW - 1:CW],
                                       ALU.mult, ALU.add).then_inc(s["scan_done"], 1)

            def add_y(g, k):
                c = g * GR + k
                wait(dve, "y1_mm", c + 1)
                mine = x1[:, bass.ds(g * (GR * CH) + k * CH, CH), :]
                dve.tensor_tensor(mine, b_y1[k % 2].rearrange("p (t d) -> p t d", t=CH), mine, ALU.add).then_inc(s["x1_sum"], 1)
                wait(dve, "x1_sum", c + 1)
                for t in range(CH):
                    tile = bass.ds(g * (GR * CH) + (k * CH + t), 1)
                    dve.bn_stats(st1[:, tile, :], x1[:, tile, :]).then_inc(s["st1_done"], 1)

            evac_x(0, 0)
            for g in range(NG):
                for k in range(GR):
                    if k + 1 < GR:
                        evac_x(g, k + 1)
                    if g > 0:
                        scan(g - 1, k)
                    positive_part(g, k)
                for k in range(GR):
                    softplus(g, k)
                if g > 0:
                    dve.wait_ge(s["ld_x"], 16 * B)
                    for k in range(GR):
                        add_y(g - 1, k)
                if g + 1 < NG:
                    evac_x(g + 1, 0)
            for k in range(GR):
                scan(NG - 1, k)
            for k in range(GR):
                add_y(NG - 1, k)
            dve.wait_ge(s["st1_done"], T)
            dve.tensor_tensor(mv1[:, :, 0], st1[:, :, 1], st1[:, :, 4], ALU.add).then_inc(s["mv1_done"], 1)
            dve.tensor_tensor(mv1[:, :, 1], st1[:, :, 1], st1[:, :, 4], ALU.subtract).then_inc(s["mv1_done"], 1)
            dve.tensor_tensor(rstd1[:, :], st1[:, :, 2], st1[:, :, 5], ALU.add).then_inc(s["mv1_done"], 1)
            dve.wait_ge(s["mv1_done"], 3)
            dve.tensor_scalar(mv1[:, :, 0], mv1[:, :, 0], 0.5, None, ALU.mult).then_inc(s["mv1_done"], 1)
            dve.scalar_tensor_tensor(out=mv1[:, :, 1], in0=mv1[:, :, 1], scalar=0.25, in1=mv1[:, :, 1],
                                     op0=ALU.mult, op1=ALU.mult).then_inc(s["mv1_done"], 1)
            dve.wait_ge(s["mv1_done"], 5)
            dve.scalar_tensor_tensor(out=mv1[:, :, 1], in0=rstd1[:, :], scalar=1.0 / D, in1=mv1[:, :, 1],
                                     op0=ALU.mult, op1=ALU.add).then_inc(s["mv1_done"], 1)
            dve.wait_ge(s["sd1"], 1)
            dve.reciprocal(rstd1[:, :], rstd1[:, :]).then_inc(s["rstd1_done"], 1)
            dve.wait_ge(s["rstd1_done"], 1)

            def norm_x1(g, k):
                wait(dve, "x1T_mm", g * GR + (k + 1 - GR))
                wait(dve, "x1_copy", g * GR + (k + 1 - GR))
                for t in range(CH):
                    n = g * (GR * CH) + (k * CH + t)
                    last = dve.tensor_scalar(xs[:, k, t:t + 1, :], x1[:, bass.ds(n, 1), :], mv1[:, bass.ds(n, 1), 0],
                                             rstd1[:, bass.ds(n, 1)], ALU.subtract, ALU.mult)
                last.then_inc(s["nrm"], 1)

            def batch_stats(g, k):
                wait(dve, "x1T_evac", g * GR + (k + 1))
                dve.bn_stats(bst[:, bass.ds(g * GR + k, 1), :], b_x1T[k]).then_inc(s["bst_done"], 1)

            def norm_group(g):
                for k in range(GR):
                    norm_x1(g, k)
                    if k >= 2:
                        batch_stats(g, k - 2)
                batch_stats(g, GR - 2)
                batch_stats(g, GR - 1)

            norm_group(0)
            with dve.Fori(1, NG) as g:
                norm_group(g)
            dve.wait_ge(s["bst_done"], NCH)
            dve.bn_aggr(bmv[:, :], bst[:, :, :]).then_inc(s["bmv_done"], 1)
            dve.wait_ge(s["bsd_done"], 1)
            dve.reciprocal(bsd[:, :], bsd[:, :]).then_inc(s["bsd_inv"], 1)
            dve.wait_ge(s["bsd_inv"], 1)
            dve.tensor_tensor(bsc[:, 0:1], bsd[:, :], cols[:, 1:2], ALU.mult).then_inc(s["bsc_half"], 1)
            dve.wait_ge(s["bsc_half"], 1)
            dve.tensor_tensor(bsd[:, :], bsc[:, 0:1], bmv[:, 0:1], ALU.mult).then_inc(s["bsc_mu"], 1)
            dve.wait_ge(s["bsc_mu"], 1)
            dve.tensor_tensor(bsc[:, 1:2], cols[:, 2:3], bsd[:, :], ALU.subtract).then_inc(s["bsc_done"], 1)

            def hot_slice(hf):
                return slice(32 * hf, 32 * hf + 32)

            def spread(f, hf):
                v = listsT[:, f, 64 * hf:64 * hf + 64].rearrange("p (g s) -> p g s", s=2)
                return v.unsqueeze(2).to_broadcast([P, 32, NK, 2])

            def hot_y(m, hf):
                wait(dve, "lists_evac", m + 1)
                wait(dve, "hotlo_done", m * 2 - 1 + hf)
                dve.tensor_tensor(hoty[:, hot_slice(hf)], iota[:, 1].unsqueeze(1).to_broadcast([P, 32, NK, 2]),
                                  spread(1, hf), ALU.is_equal).then_inc(s["hoty_done"], 1)

            def hot_x(m, par, hf):
                wait(dve, "p_mm", m * 2 - 3 + hf)
                dve.tensor_tensor(hotx[:, par, hot_slice(hf)], iota[:, 0].unsqueeze(1).to_broadcast([P, 32, NK, 2]),
                                  spread(0, hf), ALU.is_equal)

            def hot_w(m, par, hf):
                wait(dve, "hoty_done", m * 2 + (hf + 1))
                dve.tensor_tensor(hotw[:, par, 0, hot_slice(hf)], hoty[:, hot_slice(hf)], spread(2, hf),
                                  ALU.mult).then_inc(s["hot_done"], 1)

            def step(m, hot_par, hot_before, norm_quad=None, scaled=True):
                for t in range(2):
                    hold(dve, "sims_ready", m * 2 + (t + 1))
                    for r in range(ROWS):
                        p, h = r // H, r % H
                        last = dve.max(vals[:, p, t * H + h, :], sims[:, t, r, :])
                    last.then_inc(s["vals_done"], 1)
                wait(dve, "code_done", m)
                for t in range(2):
                    hold(dve, "vals_done", m * 2 + (t + 1))
                    for r in range(ROWS):
                        p, h = r // H, r % H
                        last = dve.max_index(idx[:, p, t * H + h, :], vals[:, p, t * H + h, :], sims[:, t, r, :])
                    last.then_inc(s["idx_done"], 1)
                if hot_before:
                    hot_y(m - 1, 0)
                    hot_x(m - 1, hot_par, 0)
                hold(dve, "cand_done", m + 1)
                for r in range(RH):
                    last = dve.max(top[:, r, :], cand[:, r, :])
                last.then_inc(s["top_done"], 1)
                if hot_before:
                    hot_w(m - 1, hot_par, 0)
                    hot_y(m - 1, 1)
                hold(dve, "top_done", m + 1)
                for r in range(RH):
                    last = dve.match_replace(marked[:, r, :], top[:, r, :], cand[:, r, :], REPLACED)
                last.then_inc(s["marked_done"], 1)
                if hot_before:
                    hot_x(m - 1, hot_par, 1)
                wait(dve, "code_done", m + 1)
                wait(dve, "marked_done", m + 1)
                dve.scalar_tensor_tensor(
                    out=words16[:, 0, :, 1],
                    in0=marked[:, :, :].rearrange("p h c -> p (h c)"), scalar=REPLACED / 2,
                    in1=code[:, :, :].rearrange("p h c -> p (h c)"),
                    op0=ALU.is_lt, op1=ALU.mult).then_inc(s["hi_done"], 1)
                if hot_before:
                    hot_w(m - 1, hot_par, 1)
                if norm_quad is not None:
                    residual(norm_quad)
                wait(dve, "lo_done", m + 1)
                hold(dve, "hi_done", m + 1)
                for w in range(2):
                    if w == 1:
                        hold(dve, "hi2_done", m + 1)
                    for r in range(RH):
                        last = dve.max(picked[:, w, r, :], words[:, w, r, :])
                last.then_inc(s["picked_done"], 1)
                wait(dve, "conv_done", m)
                wait(dve, "picked_done", m + 1)
                dve.tensor_copy(exk16, picked16[:, :, :, 0]).then_inc(s["exk_done"], 1)
                dve.tensor_scalar(codes[:, 0, :], picked16[:, 0, :, 1], NK * (NK - 1), None, ALU.bitwise_and)
                if norm_quad is not None and scaled:
                    scales(norm_quad)
                wait(dve, "exk_done", m + 1)
                dve.reduce_sum(zsum[:, :], exk[:, :, :], AX_X).then_inc(s["z_done"], 1)
                dve.tensor_scalar(codes[:, 1, :], picked16[:, 0, :, 1], NK - 1, None,
                                  ALU.bitwise_and).then_inc(s["codes_done"], 1)
                wait(dve, "z_done", m + 1)
                dve.reciprocal(zinv[:, :], zsum[:, :]).then_inc(s["zinv_done"], 1)
                wait(dve, "zinv_done", m + 1)
                wait(dve, "wlo_done", m)
                dve.scalar_tensor_tensor(out=wk[:, :, :], in0=exk[:, :, :], scalar=W_SCALE,
                                         in1=zinv[:, :].unsqueeze(2).to_broadcast([P, RH, TOPK]), op0=ALU.mult,
                                         op1=ALU.mult).then_inc(s["wk_done"], 1)

            def residual(q, y2=b_y2):
                wait(dve, "out_done", q)
                wait(dve, "y2_mm", q + 1)
                dve.tensor_tensor(zf[:, :, :], y2.rearrange("p (t d) -> p t d", t=CH), x1[:, bass.ds(q * CH, CH), :],
                                  ALU.add).then_inc(s["zf_done"], 1)
                wait(dve, "zf_done", q + 1)
                for t in range(CH):
                    last = dve.bn_stats(st2[:, t, :], zf[:, t, :])
                last.then_inc(s["st2_done"], 1)
                hold(dve, "st2_done", q + 1)
                for t in range(CH):
                    last = dve.bn_aggr(mv2[:, t, :], st2[:, t, :])
                last.then_inc(s["mv2_done"], 1)

            def scales(q):
                wait(dve, "sd2", q + 1)
                dve.reciprocal(rstd2[:, :], rstd2[:, :]).then_inc(s["rstd2_done"], 1)
                wait(dve, "rstd2_done", q + 1)
                dve.scalar_tensor_tensor(out=nmr2[:, :], in0=mv2[:, :, 0], scalar=-1.0, in1=rstd2[:, :],
                                         op0=ALU.mult, op1=ALU.mult).then_inc(s["nmr2_done"], 1)

            def quad(q, before, before2, scaled=True):
                step(q * 2, 1, before)
                step(q * 2 + 1, 0, True, q - 2 if before2 else None, scaled)

            quad(0, False, False)
            quad(1, True, False)
            quad(2, True, True)
            with dve.Fori(3, NCH - 1) as q:
                quad(q, True, True)
            quad(NCH - 1, True, True, scaled=False)
            for hf in range(2):
                hot_y(T // 2 - 1, hf)
                hot_x(T // 2 - 1, 1, hf)
                hot_w(T // 2 - 1, 1, hf)
            dve.wait_ge(s["relaid"], 256 * (NCH - 1))
            for jh in range(JH):
                dve.wait_ge(s["gelu_done"], (NCH - 2) * JH + (jh + 1))
                by_token = gl[:, jh].rearrange("p (n c) -> p n c", c=4)
                dve.tensor_tensor(by_token, pt[:, jh].rearrange("p (c n) -> p n c", c=4), by_token,
                                  ALU.mult).then_inc(s["a_last"], 1)
            scales(NCH - 3)
            residual(NCH - 2)
            scales(NCH - 2)
            dve.wait_ge(s["relaid"], 256 * NCH)
            dve.wait_ge(s["gelu_done"], JH * NCH)
            for t in range(CH):
                at = slice(t * P, (t + 1) * P)
                by_token = gl_last[:, :, at].rearrange("p j (n c) -> p j n c", c=4)
                dve.tensor_tensor(by_token, pt.rearrange("p j (c t n) -> p j t n c", c=4, t=CH)[:, :, t], by_token,
                                  ALU.mult).then_inc(s["tile_done"], 1)
            residual(NCH - 1, psum[:, 0:512])
            scales(NCH - 1)

        @block.tensor
        def _(pe):
            def weights(g):
                lo, hi = W_GROUPS[g]
                for n in range(lo, hi):
                    last = pe.transpose(b_w[g][:, (n - lo) * P:(n - lo + 1) * P], nat[:, n, :], ident[:, :])
                last.then_inc(s["w_trn"], 1)

            def turn_x(g, k):
                wait(pe, f"ld_x{k}", g * 16 + 16)
                wait(pe, "xT_evac", g * GR + k)
                for t in range(CH):
                    last = pe.transpose(b_xT[:, t * P:(t + 1) * P], xs[:, k, t, :], ident[:, :])
                last.then_inc(s["xT_mm"], 1)

            def project(g, k, which):
                c = g * GR + k
                wait(pe, "xT_evac", c + 1)
                for n in which:
                    to, done, used, uses = (
                        (b_delta[k % 2], "z_delta", "relu_done", c - 1), (b_in, "z_in", "tin_done", c),
                        (b_sel, "z_sel", "sel_done", c), (b_gate, "z_gate", "gate_done", c))[n]
                    wait(pe, used, uses)
                    pe.matmul(to, trn[:, n, :], xT[:, k], start=True, stop=True).then_inc(s[done], 1)

            def project_out(g, k):
                c = g * GR + k
                wait(pe, "gated", c + 1)
                wait(pe, "x1_sum", c - 1)
                for t in range(CH):
                    last = pe.matmul(b_y1[k % 2][:, t * P:(t + 1) * P], outg[:, k, t * P:(t + 1) * P], trn[:, 4, :],
                                     start=True, stop=True)
                last.then_inc(s["y1_mm"], 1)

            pe.wait_ge(s["c_ident"], 2)
            turn_x(0, 0)
            pe.wait_ge(s["ld_w"], 64)
            weights(0)
            pe.wait_ge(s["w_evac"], 1)
            for g in range(NG):
                for k in range(GR):
                    if k + 1 < GR:
                        turn_x(g, k + 1)
                    project(g, k, (0, 1))
                if g == 0:
                    pe.wait_ge(s["ld_wout"], 16)
                    weights(1)
                else:
                    pe.wait_ge(s["w_evac"], 2)
                    for k in range(2):
                        project_out(g - 1, k)
                for k in range(GR):
                    project(g, k, (2, 3))
                if g + 1 < NG:
                    turn_x(g + 1, 0)
                for k in range(2, GR if g else 0):
                    project_out(g - 1, k)
            pe.wait_ge(s["ld_keys"], 16 * 11)
            pe.wait_ge(s["relu_done"], NCH)
            for g in range(2, 5):
                weights(g)
            for k in range(GR):
                project_out(NG - 1, k)
            pe.wait_ge(s["w_evac"], 5)
            for r in range(ROWS):
                p, h = r // H, r % H
                last = pe.matmul(b_m[:, r * NK:(r + 1) * NK], wq[:, r, :],
                                 trn[:, 5 + 2 * (h // 4) + p, (h % 4) * NK:(h % 4 + 1) * NK], start=True, stop=True)
            last.then_inc(s["m_mm"], 1)

            def turn_x1(g):
                for k in range(GR):
                    wait(pe, "nrm", g * GR + (k + 1))
                    wait(pe, "bst_done", g * GR + (k + 1 - GR))
                    for t in range(CH):
                        last = pe.transpose(b_x1T[k][:, t * P:(t + 1) * P], xs[:, k, t, :], ident[:, :])
                    last.then_inc(s["x1T_mm"], 1)

            turn_x1(0)
            with pe.Fori(1, NG) as g:
                turn_x1(g)
            pe.wait_ge(s["m_evac"], 1)
            pe.wait_ge(s["x1T_evac"], NCH)

            def scores(m):
                for t in range(2):
                    wait(pe, "xn_done", m * 2 + (t + 1))
                    wait(pe, "sims_ready", m * 2 - 1 + t)
                    pe.matmul(b_sim[t], xn[:, t], msim[:, :], start=True, stop=True).then_inc(s["sim_mm"], 1)

            def lists_turned(m):
                wait(pe, "conv_done", m + 1)
                wait(pe, "wlo_done", m + 1)
                wait(pe, "lists_evac", m)
                for f in range(4):
                    last = pe.transpose(b_lists[:, f * P:(f + 1) * P], lists[:, f, :], ident16[:, :])
                last.then_inc(s["lists_mm"], 1)

            def scatter(m, par, hf):
                wait(pe, "p_evac", m * 4 + 2 * hf)
                wait(pe, "hot_done", m * 2 + (hf + 1))
                hold(pe, "hotlo_done", m * 2 + (hf + 1))
                for k in range(16):
                    for e in range(2):
                        two = slice(32 * hf + 2 * k, 32 * hf + 2 * k + 2)
                        for tile in range(2):
                            rows = slice(64 * tile, 64 * tile + 64)
                            at = 1024 * tile + 2 * NK * k
                            for part in range(2):
                                last = pe.matmul(psum[64 * e:64 * e + 64, at:at + 2 * NK],
                                                 hotx[rows, par, two, :, e].rearrange("p b i -> p (b i)"),
                                                 hotw[rows, par, part, two, :, e].rearrange("p b j -> p (b j)"),
                                                 start=(part == 0), stop=(part == 1))
                last.then_inc(s["p_mm"], 1)

            def experts_in(q, banks=b_g, lists_before=None, jhs=range(JH)):
                n = len(banks)
                if banks is b_g:
                    wait(pe, "zf_done", q)
                    wait(pe, "lists_evac", lists_before)
                for jh in jhs:
                    if jh >= n or jhs is HALF:
                        wait(pe, "gelu_done", q * JH + (jh + 1 - n))
                    pe.matmul(banks[jh % n], trn[:, 9 + jh, :],
                              x1T[:, bass.ds(q * CW, CW)], start=True, stop=True).then_inc(s["g_mm"], 1)

            def experts_out(q, to=b_y2, a=gl, weighed="a_done", jhs_weighed=None):
                if jhs_weighed is not None:
                    wait(pe, weighed, jhs_weighed)
                for t in range(CH):
                    if jhs_weighed is None:
                        wait(pe, weighed, t + 1)
                    for jh in range(JH):
                        last = pe.matmul(to[:, t * P:(t + 1) * P],
                                         a[:, jh, t * P:(t + 1) * P], ko[:, jh, :], start=(jh == 0), stop=(jh == JH - 1))
                last.then_inc(s["y2_mm"], 1)

            def quad(q, before, before2, last=False):
                if before:
                    lists_turned(q * 2 - 1)
                scores(q * 2 + 1)
                if before2:
                    experts_in(q - 2, lists_before=q * 2)
                if before:
                    scatter(q * 2 - 1, 1, 0)
                    scatter(q * 2 - 1, 1, 1)
                if before2:
                    wait(pe, "gelu_done", (q - 1) * JH)
                lists_turned(q * 2)
                if not last:
                    scores(q * 2 + 2)
                if before2:
                    experts_out(q - 2, jhs_weighed=(q - 1) * JH)
                scatter(q * 2, 0, 0)
                if last:
                    pe.wait_ge(s["sims_ready"], T)
                    experts_in(q - 1, b_sim, jhs=HALF)
                scatter(q * 2, 0, 1)

            scores(0)
            quad(0, False, False)
            quad(1, True, False)
            quad(2, True, True)
            with pe.Fori(3, NCH - 1) as q:
                quad(q, True, True)
            quad(NCH - 1, True, True, last=True)
            lists_turned(T // 2 - 1)
            experts_in(NCH - 2, b_sim, jhs=REST)
            scatter(T // 2 - 1, 1, 0)
            experts_in(NCH - 1, b_sim, jhs=HALF)
            scatter(T // 2 - 1, 1, 1)
            experts_in(NCH - 1, b_sim, jhs=REST)
            experts_out(NCH - 2, weighed="a_last", jhs_weighed=JH)
            pe.wait_ge(s["p_evac"], NCH * 8)
            experts_out(NCH - 1, psum[:, 0:512], gl_last, "tile_done")


_INS = ['L0_attn_x', 'L0_attn_W_in', 'L0_attn_W_select', 'L0_attn_W_gate', 'L0_attn_W_out', 'L0_attn_W_delta',
        'L0_attn_log_a', 'L0_ffn_gamma', 'L0_ffn_beta', 'L0_ffn_w_q', 'L0_ffn_keys', 'L0_ffn_key_in',
        'L0_ffn_key_out']


def kernel(**inputs):
    import numpy as _np
    import concourse.bacc as _bacc
    from concourse import mybir as _mybir
    from concourse.bass_utils import run_bass_kernel_spmd as _run

    nc = _bacc.Bacc("TRN2", target_bir_lowering=False, num_devices=1)
    arrays, args = {}, []
    for name in _INS:
        a = _np.ascontiguousarray(inputs[name])
        arrays[f"in_{name}_dram"] = a
        args.append(nc.dram_tensor(f"in_{name}_dram", a.shape, _mybir.dt.from_np(a.dtype), kind="ExternalInput").ap())
    shape = inputs['L0_attn_x'].shape
    args.append(nc.dram_tensor("out_0_dram", shape, _mybir.dt.float32, kind="ExternalOutput").ap())
    seqffn_kernel(nc, *args)
    r = _run(nc, [arrays], core_ids=[0])
    return r.results[0]["out_0_dram"]
```
